# Optimizing a Trainium2 kernel written in Bass

```python
import numpy as np
import jax
import jax.numpy as jnp

def _softmax(x, axis=-1):
    return jax.nn.softmax(x, axis=axis)

def _gelu(x):
    return jax.nn.gelu(x, approximate=True)

def _silu(x):
    return jax.nn.silu(x)

def _sigmoid(x):
    return jax.nn.sigmoid(x)

def _layernorm(x, axis=-1, eps=1e-05):
    m = jnp.mean(x, axis=axis, keepdims=True)
    v = jnp.var(x, axis=axis, keepdims=True)
    return (x - m) / jnp.sqrt(v + eps)

def _scatter_add(tgt, idx, src, axis=0):
    return tgt.at[idx].add(src)

def _segment_sum(src, seg, n):
    return jax.ops.segment_sum(src, seg, n)
kernel_name = 'mk_flamingo_gated_d1_seqx_r4_9298f4'

def setup_inputs(seed: int=0):
    np.random.seed(seed)
    _w = jnp.asarray

    def _rec_inputs():
        import jax
        import jax.numpy as jnp
        _rk = jax.random.key(seed)
        x = -0.0002928 + 1 * jax.random.normal(jax.random.fold_in(_rk, 1), (1, 2048, 256), jnp.float32)
        _lenS = 2048 - jax.random.randint(jax.random.fold_in(_rk, 7), (1,), 0, max(1, 2048 // 4) + 1, jnp.int32)
        _lenS2 = 1601 - jax.random.randint(jax.random.fold_in(_rk, 8), (1,), 0, max(1, 1601 // 4) + 1, jnp.int32)
        _ctx_1024P = jax.random.normal(jax.random.fold_in(_rk, 11), (1, 16, 256), jnp.float32)
        _ctx_1024c = jax.random.dirichlet(jax.random.fold_in(_rk, 511), 0.3 * jnp.ones((16,), jnp.float32), (1, 1601))
        _ctx_1024t = jnp.einsum('bsk,bkd->bsd', _ctx_1024c, _ctx_1024P)
        _ctx_1024t = _ctx_1024t * jax.lax.rsqrt(jnp.mean(jnp.square(_ctx_1024t)) + 1e-12) * 0.953939
        ctx_1024 = -1.39393e-06 + 0.999914 * (_ctx_1024t + 0.3 * jax.random.normal(jax.random.fold_in(_rk, 611), (1, 1601, 256), jnp.float32))
        _g = jax.random.normal(jax.random.fold_in(_rk, 9001), (2, 1), jnp.float32)
        _g = jnp.sign(_g) * jnp.maximum(jnp.abs(_g), 1.0) + (_g == 0) * 1.0
        g_xattn = _g[0]
        g_ffn = _g[1]
        return (x, ctx_1024, g_xattn, g_ffn)
    x, ctx_1024, g_xattn, g_ffn = _rec_inputs()

    def _L0_xattn_setup():
        import jax, jax.numpy as jnp
        import numpy as np
        DIM = 256
        NUM_HEADS = 16
        HEAD_DIM = DIM // NUM_HEADS
        key = jax.random.key(seed)
        ks = jax.random.split(key, 11)
        B, N, C = (2, 512, DIM)
        s = 1.0 / np.sqrt(C)
        inp = {'q': jax.random.normal(ks[0], (B, N, C), jnp.float32), 'k': jax.random.normal(ks[1], (B, N, C), jnp.float32), 'v': jax.random.normal(ks[2], (B, N, C), jnp.float32), 'Wq': jax.random.normal(ks[3], (C, C), jnp.float32) * s, 'bq': jnp.zeros((C,), jnp.float32), 'Wk': jax.random.normal(ks[4], (C, C), jnp.float32) * s, 'bk': jnp.zeros((C,), jnp.float32), 'Wv': jax.random.normal(ks[5], (C, C), jnp.float32) * s, 'bv': jnp.zeros((C,), jnp.float32), 'Wo': jax.random.normal(ks[6], (C, C), jnp.float32) * s, 'bo': jnp.zeros((C,), jnp.float32)}
        return inp
    _L0_xattn_all = _L0_xattn_setup()
    _L0_xattn_in = {k: v for k, v in _L0_xattn_all.items() if k in ('Wq', 'bq', 'Wk', 'bk', 'Wv', 'bv', 'Wo', 'bo')}
    del _L0_xattn_all

    def _L0_ffn_setup():
        import jax, jax.numpy as jnp
        import numpy as np
        B, S, H, I, SI, E, TOPK = (2, 256, 256, 128, 512, 8, 2)
        key = jax.random.key(seed)
        ks = jax.random.split(key, 8)
        w = 0.02
        return {'hidden_states': jax.random.normal(ks[0], (B, S, H), jnp.float32), 'router_weight': jax.random.normal(ks[1], (E, H), jnp.float32) * w, 'gate_up_proj': jax.random.normal(ks[2], (E, 2 * I, H), jnp.float32) * w, 'down_proj': jax.random.normal(ks[3], (E, H, I), jnp.float32) * w, 'shared_gate_w': jax.random.normal(ks[4], (SI, H), jnp.float32) * w, 'shared_up_w': jax.random.normal(ks[5], (SI, H), jnp.float32) * w, 'shared_down_w': jax.random.normal(ks[6], (H, SI), jnp.float32) * w, 'shared_expert_gate_w': jax.random.normal(ks[7], (1, H), jnp.float32) * w}
    _L0_ffn_all = _L0_ffn_setup()
    _L0_ffn_in = {k: v for k, v in _L0_ffn_all.items() if k in ('router_weight', 'gate_up_proj', 'down_proj', 'shared_gate_w', 'shared_up_w', 'shared_down_w', 'shared_expert_gate_w')}
    del _L0_ffn_all
    return {'x': x, 'ctx_1024': ctx_1024, 'g_xattn': g_xattn, 'g_ffn': g_ffn, 'L0_xattn_Wq': _L0_xattn_in['Wq'], 'L0_xattn_bq': _L0_xattn_in['bq'], 'L0_xattn_Wk': _L0_xattn_in['Wk'], 'L0_xattn_bk': _L0_xattn_in['bk'], 'L0_xattn_Wv': _L0_xattn_in['Wv'], 'L0_xattn_bv': _L0_xattn_in['bv'], 'L0_xattn_Wo': _L0_xattn_in['Wo'], 'L0_xattn_bo': _L0_xattn_in['bo'], 'L0_ffn_router_weight': _L0_ffn_in['router_weight'], 'L0_ffn_gate_up_proj': _L0_ffn_in['gate_up_proj'], 'L0_ffn_down_proj': _L0_ffn_in['down_proj'], 'L0_ffn_shared_gate_w': _L0_ffn_in['shared_gate_w'], 'L0_ffn_shared_up_w': _L0_ffn_in['shared_up_w'], 'L0_ffn_shared_down_w': _L0_ffn_in['shared_down_w'], 'L0_ffn_shared_expert_gate_w': _L0_ffn_in['shared_expert_gate_w']}

def reference(x, ctx_1024, g_xattn, g_ffn, L0_xattn_Wq, L0_xattn_bq, L0_xattn_Wk, L0_xattn_bk, L0_xattn_Wv, L0_xattn_bv, L0_xattn_Wo, L0_xattn_bo, L0_ffn_router_weight, L0_ffn_gate_up_proj, L0_ffn_down_proj, L0_ffn_shared_gate_w, L0_ffn_shared_up_w, L0_ffn_shared_down_w, L0_ffn_shared_expert_gate_w):
    import jax
    import jax.numpy as jnp

    def _L0_xattn_ref(q, k, v, Wq, bq, Wk, bk, Wv, bv, Wo, bo):
        import jax, jax.numpy as jnp
        import numpy as np
        DIM = 256
        NUM_HEADS = 16
        HEAD_DIM = DIM // NUM_HEADS
        B, Nq, C = q.shape
        Nkv = k.shape[1]
        H, D = (NUM_HEADS, HEAD_DIM)
        qh = (q @ Wq.T + bq).reshape(B, Nq, H, D).transpose(0, 2, 1, 3)
        kh = (k @ Wk.T + bk).reshape(B, Nkv, H, D).transpose(0, 2, 1, 3)
        vh = (v @ Wv.T + bv).reshape(B, Nkv, H, D).transpose(0, 2, 1, 3)
        scale = D ** (-0.5)
        attn = jax.nn.softmax(jnp.einsum('bhqd,bhkd->bhqk', qh, kh) * scale, axis=-1)
        out = jnp.einsum('bhqk,bhkd->bhqd', attn, vh)
        out = out.transpose(0, 2, 1, 3).reshape(B, Nq, C)
        return out @ Wo.T + bo

    def _L0_ffn_ref(hidden_states, router_weight, gate_up_proj, down_proj, shared_gate_w, shared_up_w, shared_down_w, shared_expert_gate_w):
        import jax, jax.numpy as jnp
        import numpy as np
        B, S, H, I, SI, E, TOPK = (2, 256, 256, 128, 512, 8, 2)
        b, s, h = hidden_states.shape
        x = hidden_states.reshape(-1, h)
        shared = jax.nn.silu(x @ shared_gate_w.T) * (x @ shared_up_w.T) @ shared_down_w.T
        logits = x @ router_weight.T
        probs = jax.nn.softmax(logits.astype(jnp.float32), axis=-1)
        top_v, top_i = jax.lax.top_k(probs, TOPK)
        top_v = (top_v / jnp.sum(top_v, axis=-1, keepdims=True)).astype(logits.dtype)
        cw = jnp.sum(jax.nn.one_hot(top_i, E, dtype=top_v.dtype) * top_v[..., None], axis=1)
        gu = jnp.einsum('th,eih->eti', x, gate_up_proj)
        gate, up = jnp.split(gu, 2, axis=-1)
        act = jax.nn.silu(gate) * up
        per_expert = jnp.einsum('eti,ehi->eth', act, down_proj)
        expert_out = jnp.einsum('eth,te->th', per_expert, cw)
        out = expert_out + jax.nn.sigmoid(x @ shared_expert_gate_w.T) * shared
        return out.reshape(b, s, h)
    x = x + jnp.tanh(g_xattn[0]) * _L0_xattn_ref(_layernorm(x, axis=-1), ctx_1024, ctx_1024, L0_xattn_Wq, L0_xattn_bq, L0_xattn_Wk, L0_xattn_bk, L0_xattn_Wv, L0_xattn_bv, L0_xattn_Wo, L0_xattn_bo)
    x = x + jnp.tanh(g_ffn[0]) * _L0_ffn_ref(_layernorm(x, axis=-1), L0_ffn_router_weight, L0_ffn_gate_up_proj, L0_ffn_down_proj, L0_ffn_shared_gate_w, L0_ffn_shared_up_w, L0_ffn_shared_down_w, L0_ffn_shared_expert_gate_w)
    return x

_drawn_inputs = setup_inputs


def setup_inputs(seed=0):
    import zlib

    import numpy as np

    out = dict(_drawn_inputs(seed))
    spreads = {'L0_xattn_bq': (0.0, 0.513),
     'L0_xattn_bk': (0.0, 0.8),
     'L0_xattn_bv': (0.0, 0.1),
     'L0_xattn_bo': (0.0, 0.1)}
    factors = {'L0_ffn_router_weight': 8.0,
     'L0_ffn_gate_up_proj': 7.652,
     'L0_ffn_down_proj': 7.667,
     'L0_ffn_shared_gate_w': 5.346,
     'L0_ffn_shared_up_w': 5.258,
     'L0_ffn_shared_down_w': 5.252,
     'L0_ffn_shared_expert_gate_w': 8.0}
    for name, (base, spread) in spreads.items():
        noise = np.random.default_rng([zlib.crc32(name.encode()), seed]).standard_normal(out[name].shape)
        drawn = base * np.exp(spread * noise) if base else spread * noise
        out[name] = jnp.asarray(drawn.astype(out[name].dtype))
    for name, factor in factors.items():
        out[name] = (out[name] * factor).astype(out[name].dtype)
    return out
```

```python
from contextlib import ExitStack

import concourse.bass as bass
from concourse import mybir

F32 = mybir.dt.float32
BF16 = mybir.dt.bfloat16
U32 = mybir.dt.uint32
ALU = mybir.AluOpType
ACT = mybir.ActivationFunctionType
AX = mybir.AxisListType

P = 128
C = 256
NT = 2048
NK = 1601
H, D = 16, 16
HG = 4
G = H // HG
QC = 512
NC = NT // QC
QT = QC // P
STEPS = G * NC
KT = -(-NK // P)
KW = [min(P, NK - P * k) for k in range(KT)]
KC = 4
KP0 = [401 * j - max(0, j - 1) for j in range(KC)]
KPW = [401] + [400] * (KC - 1)
SPLIT = 6 * D
ROWS = SPLIT + 2
VW = 32
SCALE = D ** -0.5
EPS = 1e-5
E, I, SI = 8, 128, 512
UNITS = E + SI // P
PAIRS = UNITS // 2

FILLS = QT * HG * KC + HG
EXPS = KT * HG
Q_PARTS = [0, 0, 0, 1, 1, 2]
K_PARTS = [0, 1, 2, 0, 1, 0]


def pass_a_fills():
    out, due = [], []
    for i in range(HG * QT * KC):
        out.append(("score", i // KC, i % KC))
        if (i + 1) % (QT * KC) == 0:
            due.append((i + 4, i // (QT * KC)))
        if due and i == due[0][0]:
            out.append(("shift", due.pop(0)[1], 0))
    return out + [("shift", h, 0) for _, h in due]


A_FILLS = pass_a_fills()
A_SHARE = [6, 6, 5, 6, 6, 5, 6, 6, 5, 6, 5, 5, 1]
assert sum(A_SHARE) == FILLS == len(A_FILLS)
SHIFT_AT = [A_FILLS.index(("shift", h, 0)) for h in range(HG)]


def wait(eng, sem, value):
    if not (isinstance(value, int) and value <= 0):
        eng.wait_ge(sem, value)


def hold(eng, sem, value, passed):
    eng.wait_ge(sem, value)
    eng.sem_inc(passed, 1)


def flamingo_block(nc, x, ctxT, wq, wk, wv, wo, bq, bk, bv, bo, g_x, g_f, router, gu, dw, sg, su, sd, out):
    with ExitStack() as ctx:
        def sb(name, shape, dt=F32):
            return ctx.enter_context(nc.sbuf_tensor(name, shape, dt))

        def sem(name):
            return ctx.enter_context(nc.semaphore(name))

        SPLITW = 3 * 2 * NT + 3 * 2 * NK
        parts = sb("split_parts", [P, SPLITW + 2], BF16)
        q_part = [parts[:, 2 * NT * i:2 * NT * (i + 1)].rearrange("p (a n) -> p a n", a=2) for i in range(3)]
        k_part = [parts[:, 6 * NT + 2 * NK * i:6 * NT + 2 * NK * (i + 1)].rearrange("p (a n) -> p a n", a=2)
                  for i in range(3)]
        ffw = parts[:, 0:SPLITW // 2 * 2].bitcast(F32)
        gu_w = ffw[:, 0:4096].rearrange("p (a n) -> p a n", a=2)
        dw_w = ffw[:, 4096:6144].rearrange("p (e n) -> p e n", e=E)
        sg_w = ffw[:, 6144:7168].rearrange("p (a n) -> p a n", a=2)
        su_w = ffw[:, 7168:8192].rearrange("p (a n) -> p a n", a=2)
        sd_w = ffw[:, 8192:9216].rearrange("p (e n) -> p e n", e=SI // P)

        VG = KT * HG * VW
        v_mem = sb("v_all", [P, G * VG])
        v_all = v_mem[:, :].rearrange("p (g k h w) -> p g k h w", g=G, k=KT, h=HG)
        v_grp = [sb(f"v_group{i}", [P, VG]) for i in range(2)]
        v_use = [v[:, :].rearrange("p (k h w) -> p k h w", k=KT, h=HG) for v in v_grp]
        TW = QT * C
        xb = v_mem[:, 0:TW].rearrange("p (t n) -> p t n", t=QT)
        res = v_mem[:, TW:2 * TW].rearrange("p (t n) -> p t n", t=QT)
        xn2 = v_mem[:, 2 * TW:3 * TW].rearrange("p (t n) -> p t n", t=QT)
        att = v_mem[:, 3 * TW:4 * TW].rearrange("p (t n) -> p t n", t=QT)
        attT = v_mem[:, 4 * TW:5 * TW].rearrange("p (a n) -> p a n", a=2)

        KSW = HG * NK
        k_stack = sb("k_stack", [P, 2 * KSW], BF16)
        q_stack = sb("q_stack", [P, NC * HG * QC], BF16)
        probs = sb("probs", [P, 2, HG, QC])
        big = sb("attention_out", [P, STEPS * QC])
        x_in = big[:, 0:16 * C].rearrange("p (t n) -> p t n", t=16)
        ctx_in = big[:, 16 * C:16 * C + 2 * NK].rearrange("p (a n) -> p a n", a=2)
        temp = sb("temp", [P, 2 * NK + 2 * QC])
        k_full = temp[:, 0:2 * NK].rearrange("p (a n) -> p a n", a=2)
        q_full = temp[:, 2 * NK:2 * NK + 2 * QC].rearrange("p (a n) -> p a n", a=2)
        outT = temp[:, 0:G * QC].rearrange("p (g n) -> p g n", g=G)
        xn2T = temp[:, G * QC:G * QC + 2 * QC].rearrange("p (a n) -> p a n", a=2)
        hidden = probs[:, :, :, :].rearrange("p a b n -> p (a b) n")
        silu = v_grp[0][:, 0:2 * QC].rearrange("p (a n) -> p a n", a=2)

        xnT = sb("xnT", [P, 2, QC])
        wq_s, wk_s, wv_s, wo_s = (sb(n, [P, 2, C]) for n in ("wq", "wk", "wv", "wo"))
        bq_s, bk_s = sb("bq", [P, 2]), sb("bk", [P, 2])
        bv_s, bo_s = sb("bv", [P, C]), sb("bo", [P, C])
        rt_w = sb("router", [P, 2, E + 1])
        gates = sb("gates", [P, 2])
        tg = sb("tanh_gates", [P, 2])
        ident = sb("ident", [P, P])
        ident_b = sb("ident_b", [P, P], BF16)
        mhalf = sb("minus_half", [P, QT])
        iota = sb("iota", [P, E])
        stats = sb("stats", [P, QT, 6])
        mv1 = sb("mean_var1", [P, 16, 2])
        rstd1 = sb("rstd1", [P, 16])
        piece_max = sb("piece_max", [P, HG * QT, KC])
        neg_max = sb("neg_max", [P, HG * QT])
        shift = sb("shift_parts", [P, HG * QT, 2], BF16)
        rden = sb("rden", [P, QT, H])
        mv2 = sb("mean_var2", [P, QT, 2])
        rstd2 = sb("rstd2", [P, QT])
        rneg = sb("router_neg_max", [P, QT])
        e8 = sb("router_exp", [P, QT, E])
        ez = sb("gate_exp", [P, QT])
        v8 = sb("top_values", [P, QT, 8])
        i8 = sb("top_index", [P, QT, 8], U32)
        i2 = sb("top2_index", [P, QT, 2])
        s2 = sb("top2_sum", [P, QT])
        r2 = sb("top2_scale", [P, QT])
        w2 = sb("top2_weight", [P, QT, 2])
        cwa, cwb = sb("weights_first", [P, QT, E]), sb("weights_second", [P, QT, E])
        cw = sb("weights", [P, QT, E + 1])

        ps_a = ctx.enter_context(nc.psum_tensor("ps_a", [P, 4, 512], F32))
        ps_b = ctx.enter_context(nc.psum_tensor("ps_b", [P, 3, 512], F32))
        ps_o = ctx.enter_context(nc.psum_tensor("ps_o", [P, 512], F32))
        bank_m = [ps_b[:, 2, :], ps_o[:, :]]
        bank_d = [ps_b[:, 0, :], ps_b[:, 1, :]]

        x_loaded = [sem(f"x_loaded{c}") for c in range(NC)]
        ctx_loaded, wk_loaded, wq_loaded = sem("ctx_loaded"), sem("wk_loaded"), sem("wq_loaded")
        wv_loaded, wo_loaded = sem("wv_loaded"), sem("wo_loaded")
        consts_made, pool_chain, dve_chain = sem("consts_made"), sem("pool_chain"), sem("dve_chain")
        ln1_stats, ln1_rstd, ln1_done = sem("ln1_stats"), sem("ln1_rstd"), sem("ln1_done")
        xnT_filled, xnT_copied = sem("xnT_filled"), sem("xnT_copied")
        k_filled, k_copied, k_split = sem("k_filled"), sem("k_copied"), sem("k_split")
        q_filled, q_copied, q_split = sem("q_filled"), sem("q_copied"), sem("q_split")
        v_filled, v_copied = sem("v_filled"), sem("v_copied")
        k_staged, q_staged, v_staged = sem("k_staged"), [sem("q_staged0"), sem("q_staged1")], [sem("v_staged0"), sem("v_staged1")]
        a_filled, a_reduced, head_max = sem("a_filled"), sem("a_reduced"), sem("head_max")
        shift_high, shift_low, shift_copied = sem("shift_high"), sem("shift_low"), sem("shift_copied")
        b_filled, exp_done, pv_done, out_copied = sem("b_filled"), sem("exp_done"), sem("pv_done"), sem("out_copied")
        tanh_done, bo_scaled = sem("tanh_done"), sem("bo_scaled")
        ffw_loaded, outT_loaded, xb_loaded, xb_ready = sem("ffw_loaded"), sem("outT_loaded"), sem("xb_loaded"), sem("xb_ready")
        m_filled, att_ready, attT_ready, x1_ready = sem("m_filled"), sem("att_ready"), sem("attT_ready"), sem("x1_ready")
        ln2_stats, ln2_eps, ln2_rstd, xn2_ready = sem("ln2_stats"), sem("ln2_eps"), sem("ln2_rstd"), sem("xn2_ready")
        xn2T_ready, rneg_ready, router_exp = sem("xn2T_ready"), sem("rneg_ready"), sem("router_exp")
        gu_filled, silu_done, hidden_ready = sem("gu_filled"), sem("silu_done"), sem("hidden_ready")
        passed = {"pool": sem("pool_passed"), "dve": sem("dve_passed")}
        d_filled, combined, stored = sem("d_filled"), sem("combined"), sem("stored")

        def keys(s, h, k0, n, rows=ROWS):
            at = (s // NC) % 2 * KSW + (h * NK + k0)
            return k_stack[0:rows, at:at + n] if isinstance(at, int) else k_stack[0:rows, bass.ds(at, n)]

        def queries(s, h, q0, n, lo=0, hi=ROWS):
            at = (s % NC) * (HG * QC) + (h * QC + q0)
            return q_stack[lo:hi, at:at + n] if isinstance(at, int) else q_stack[lo:hi, bass.ds(at, n)]

        def out_at(s):
            return big[:, s * QC:(s + 1) * QC] if isinstance(s, int) else big[:, bass.ds(s * QC, QC)]

        def b_bank(i, par):
            return (i + par) % 3

        def b_bank_used(i, par):
            if i >= 3:
                return i - 2
            last = max(j for j in range(EXPS) if b_bank(j, 1 - par) == b_bank(i, par))
            return last + 1 - EXPS

        block = ctx.enter_context(nc.Block())

        @block.sync
        def _(sp):
            x_chunks = x.rearrange("(c t p) n -> c p t n", c=NC, p=P)
            sp.dma_start(wk_s[:, :, :], wk).then_inc(wk_loaded, 16)
            sp.dma_start(bk_s[:, :], bk).then_inc(wk_loaded, 16)
            sp.dma_start(x_in[:, 0:QT, :], x_chunks[0]).then_inc(x_loaded[0], 16)
            sp.dma_start(ctx_in, ctxT).then_inc(ctx_loaded, 16)
            sp.dma_start(wq_s[:, :, :], wq).then_inc(wq_loaded, 16)
            sp.dma_start(bq_s[:, :], bq).then_inc(wq_loaded, 16)
            for c in range(1, NC):
                sp.dma_start(x_in[:, QT * c:QT * (c + 1), :], x_chunks[c]).then_inc(x_loaded[c], 16)
            sp.dma_start(wv_s[:, :, :], wv).then_inc(wv_loaded, 16)
            sp.dma_start(bv_s[:, :], bv.partition_broadcast(P)).then_inc(wv_loaded, 16)
            sp.dma_start(wo_s[:, :, :], wo).then_inc(wo_loaded, 16)
            sp.dma_start(bo_s[:, :], bo.partition_broadcast(P)).then_inc(wo_loaded, 16)
            sp.dma_start(rt_w[:, :, :], router).then_inc(wo_loaded, 16)
            sp.dma_start(gates[:, 0:1], g_x.partition_broadcast(P)).then_inc(wo_loaded, 16)
            sp.dma_start(gates[:, 1:2], g_f.partition_broadcast(P)).then_inc(wo_loaded, 16)

            def stage_k(g):
                wait(sp, k_staged, 6 * 16 * g)
                for r, part in enumerate(K_PARTS):
                    src = k_part[part][64 * (g % 2):64 * (g % 2) + 64, g // 2, :]
                    dst = k_stack[D * r:D * (r + 1), g % 2 * KSW:(g % 2 + 1) * KSW]
                    sp.dma_start(dst.rearrange("p (h n) -> p h n", h=HG), src).then_inc(k_staged, 16)

            def stage_q(s):
                g, c = s // NC, s % NC
                wait(sp, q_staged[s % 2], 6 * 16 * (s // 2))
                for r, part in enumerate(Q_PARTS):
                    src = q_part[part][64 * (g % 2):64 * (g % 2) + 64, g // 2, c * QC:(c + 1) * QC]
                    dst = q_stack[D * r:D * (r + 1), c * HG * QC:(c + 1) * HG * QC]
                    sp.dma_start(dst.rearrange("p (h n) -> p h n", h=HG), src).then_inc(q_staged[s % 2], 16)

            def stage_v(s):
                g = s // NC
                wait(sp, v_staged[s % 2], 16 * (s // 2))
                sp.dma_start(v_grp[s % 2][:, :], v_mem[:, g * VG:(g + 1) * VG]).then_inc(v_staged[s % 2], 16)

            sp.wait_ge(k_split, 1)
            stage_k(0)
            sp.wait_ge(q_split, 1)
            stage_q(0)
            stage_k(1)
            for s in range(1, NC):
                sp.wait_ge(q_split, s + 1)
                stage_q(s)
            sp.wait_ge(v_copied, KT)
            sp.wait_ge(consts_made, 1)
            stage_v(0)
            stage_v(1)
            for t in range(STEPS - 2):
                sp.wait_ge(pv_done, KT * (t + 1))
                stage_v(t + 2)
                if t + NC < STEPS:
                    stage_q(t + NC)
                if t + 1 in (NC, 2 * NC):
                    stage_k((t + 1) // NC + 1)
                if t + NC == STEPS - 1:
                    sp.wait_ge(q_staged[0], 6 * 16 * STEPS // 2)
                    sp.wait_ge(q_staged[1], 6 * 16 * STEPS // 2)
                    sp.wait_ge(k_staged, 6 * 16 * G)
                    for dst, src in ((gu_w, gu), (dw_w, dw), (sg_w, sg), (su_w, su), (sd_w, sd)):
                        sp.dma_start(dst, src).then_inc(ffw_loaded, 16)
            sp.wait_ge(v_staged[0], 16 * STEPS // 2)
            sp.wait_ge(v_staged[1], 16 * STEPS // 2)

            x_c = x.rearrange("(c t p) n -> p c t n", c=NC, p=P)
            o_c = out.rearrange("(c t p) n -> p c t n", c=NC, p=P)
            big_c = big[:, :].rearrange("p (g c n) -> p g c n", g=G, c=NC)

            def of_chunk(ap, c):
                return ap[:, c, :, :] if isinstance(c, int) else ap[:, bass.ds(c, 1), :, :].squeeze(1)

            def load_chunk(c):
                wait(sp, x1_ready, QT * c)
                sp.dma_start(xb, of_chunk(x_c, c)).then_inc(xb_loaded, 16)
                if isinstance(c, int):
                    sp.wait_ge(out_copied, STEPS - NC + c + 1)
                wait(sp, att_ready, QT * c)
                sp.dma_start(outT, big_c[:, :, c, :] if isinstance(c, int) else big_c[:, :, bass.ds(c, 1), :].squeeze(2)).then_inc(outT_loaded, 16)

            def store_chunk(c):
                for t in range(QT):
                    sp.wait_ge(combined, c * QT * PAIRS + (QT * (PAIRS - 1) + t + 1))
                    sp.dma_start(of_chunk(o_c, c)[:, t, :], res[:, t, :]).then_inc(stored, 16)

            load_chunk(0)
            sp.wait_ge(out_copied, STEPS)
            with sp.Fori(1, NC) as c:
                load_chunk(c)
                store_chunk(c - 1)
            store_chunk(NC - 1)
            sp.wait_ge(stored, 16 * QT * NC)

        @block.gpsimd
        def _(pool):
            done = [0]

            def link(ins):
                done[0] += 1
                ins.then_inc(pool_chain, 1)
                pool.wait_ge(pool_chain, done[0])

            link(nc.gpsimd.memset(ident[:, :], 0.0))
            link(nc.gpsimd.affine_select(out=ident[:, :], in_=ident[:, :], compare_op=ALU.not_equal, fill=1.0,
                                         base=0, pattern=[[-1, P]], channel_multiplier=1))
            link(nc.gpsimd.tensor_copy(ident_b[:, :], ident[:, :]))
            link(nc.gpsimd.memset(mhalf[:, :], -0.5))
            for e in range(E):
                link(nc.gpsimd.memset(iota[:, e:e + 1], float(e)))
            link(nc.gpsimd.memset(k_stack[SPLIT:ROWS, :], 1.0))
            link(nc.gpsimd.memset(v_mem[:, :], 0.0))
            ones = v_mem[:, :].rearrange("p (a w) -> p a w", w=VW)[:, :, D:D + 1]
            link(nc.gpsimd.memset(ones, 1.0))
            nc.gpsimd.memset(rden[:, :, :], 0.0).then_inc(consts_made, 1)
            for c in range(NC):
                sl = slice(QT * c, QT * (c + 1))
                pool.wait_ge(ln1_stats, c + 1)
                link(nc.gpsimd.tensor_scalar(rstd1[:, sl], mv1[:, sl, 1], EPS, None, ALU.add))
                nc.gpsimd.tensor_tensor(rstd1[:, sl], rstd1[:, sl], mhalf[:, :], ALU.pow).then_inc(ln1_rstd, 1)
            pool.wait_ge(tanh_done, 1)
            nc.gpsimd.tensor_scalar(bo_s[:, :], bo_s[:, :], tg[:, 0:1], None, ALU.mult).then_inc(bo_scaled, 1)

            def shifts(s):
                for h in range(HG):
                    u = slice(QT * h, QT * (h + 1))
                    hold(pool, head_max, HG * s + (h + 1), passed["pool"])
                    nc.gpsimd.tensor_copy(shift[:, u, 0], neg_max[:, u]).then_inc(shift_high, 1)
                    pool.wait_ge(shift_high, HG * s + (h + 1))
                    nc.gpsimd.tensor_tensor(shift[:, u, 1], neg_max[:, u], shift[:, u, 0],
                                            ALU.subtract).then_inc(shift_low, 1)

            shifts(0)
            with pool.Fori(1, STEPS) as s:
                shifts(s)

            def chunk(c):
                pool.wait_ge(xb_loaded, 16 * c + 16)
                for t in range(QT):
                    nc.gpsimd.tensor_tensor(xb[:, t, :], xb[:, t, :], bo_s[:, :], ALU.add).then_inc(xb_ready, 1)
                hold(pool, ln2_stats, QT * c + QT, passed["pool"])
                nc.gpsimd.tensor_scalar(rstd2[:, :], mv2[:, :, 1], EPS, None, ALU.add).then_inc(ln2_eps, 1)
                pool.wait_ge(ln2_eps, c + 1)
                nc.gpsimd.tensor_tensor(rstd2[:, :], rstd2[:, :], mhalf[:, :], ALU.pow).then_inc(ln2_rstd, 1)

            pool.wait_ge(bo_scaled, 1)
            chunk(0)
            with pool.Fori(1, NC) as c:
                chunk(c)

        @block.scalar
        def _(act):
            def copy_k(a):
                for j in range(KC):
                    act.wait_ge(k_filled, KC * a + j + 1)
                    nc.scalar.activation(k_full[:, a, KP0[j]:KP0[j] + KPW[j]], ps_a[:, j, 0:KPW[j]], ACT.Identity,
                                         bias=bk_s[:, a:a + 1]).then_inc(k_copied, 1)

            def copy_xnT(c):
                wait(act, q_filled, 2 * c)
                for a in range(2):
                    act.wait_ge(xnT_filled, 2 * c + a + 1)
                    nc.scalar.copy(xnT[:, a, :], ps_b[:, a, :]).then_inc(xnT_copied, 1)

            def copy_q(c):
                wait(act, q_split, c)
                for a, bank in enumerate((ps_b[:, 2, :], ps_o[:, :])):
                    act.wait_ge(q_filled, 2 * c + a + 1)
                    nc.scalar.activation(q_full[:, a, :], bank, ACT.Identity,
                                         bias=bq_s[:, a:a + 1]).then_inc(q_copied, 1)

            act.wait_ge(wk_loaded, 32)
            copy_k(0)
            copy_xnT(0)
            act.wait_ge(wq_loaded, 32)
            copy_q(0)
            copy_k(1)
            for c in range(1, NC):
                copy_xnT(c)
                copy_q(c)
            act.wait_ge(wo_loaded, 16 * 5)
            nc.scalar.activation(tg[:, :], gates[:, :], ACT.Tanh).then_inc(tanh_done, 1)

            def copy_shift(s, h):
                f = SHIFT_AT[h]
                act.wait_ge(a_filled, FILLS * s + (f + 1))
                nc.scalar.copy(queries(s, h, 0, QC, SPLIT, ROWS), ps_a[SPLIT:ROWS, f % 4, :]).then_inc(shift_copied, 1)

            def copy_out(s):
                act.wait_ge(pv_done, KT * s + KT)
                nc.scalar.copy(out_at(s), ps_o[:, :]).then_inc(out_copied, 1)

            def step(s, par, next_a, first=False):
                f = 0
                for k in range(KT):
                    for h in range(HG):
                        i = HG * k + h
                        act.wait_ge(b_filled, EXPS * s + (i + 1))
                        if h == 0 and not (first and k < 2):
                            act.wait_ge(pv_done, KT * s + (k - 1))
                        nc.scalar.activation(probs[0:KW[k], (k + par) % 2, h, :], ps_b[0:KW[k], b_bank(i, par), :],
                                             ACT.Exp, scale=SCALE).then_inc(exp_done, 1)
                    if k == 0 and not first:
                        copy_out(s - 1)
                    if next_a:
                        for kind, g, _ in A_FILLS[f:f + A_SHARE[k]]:
                            if kind == "shift":
                                copy_shift(s + 1, g)
                        f += A_SHARE[k]

            for h in range(HG):
                copy_shift(0, h)
            step(0, 0, True, first=True)
            with act.Fori(0, STEPS // 2 - 1) as j:
                step(j * 2 + 1, 1, True)
                step(j * 2 + 2, 0, True)
            step(STEPS - 1, 1, False)
            copy_out(STEPS - 1)

            def chunk(c):
                for t in range(QT):
                    act.wait_ge(m_filled, M_FILLS * c + (M_AT["attT", t] + 1))
                    nc.scalar.copy(attT[:, :, t * P:(t + 1) * P],
                                   bank_m[M_AT["attT", t] % 2][:, 0:2 * P].rearrange("p (a n) -> p a n", a=2)
                                   ).then_inc(attT_ready, 1)
                for a in range(2):
                    act.wait_ge(m_filled, M_FILLS * c + (M_AT["xn2T", a] + 1))
                    nc.scalar.copy(xn2T[:, a, :], bank_m[M_AT["xn2T", a] % 2]).then_inc(xn2T_ready, 1)
                act.wait_ge(rneg_ready, c + 1)
                logits = bank_m[M_AT["router", 0] % 2][:, 0:16 * QT].rearrange("p (t e) -> p t e", t=QT)
                for t in range(QT):
                    nc.scalar.activation(e8[:, t, :], logits[:, t, 0:E], ACT.Exp, bias=rneg[:, t:t + 1])
                nc.scalar.activation(ez[:, :], logits[:, :, E], ACT.Exp, scale=-1.0).then_inc(router_exp, 1)
                for u in range(UNITS):
                    act.wait_ge(gu_filled, UNITS * c + (u + 1))
                    if not (isinstance(c, int) and c == 0 and u < 2):
                        act.wait_ge(hidden_ready, UNITS * c + (u - 1))
                    nc.scalar.activation(silu[:, u % 2, :], ps_a[:, 2 * (u % 2), :], ACT.Silu).then_inc(silu_done, 1)

            chunk(0)
            with act.Fori(1, NC) as c:
                chunk(c)

        @block.vector
        def _(dve):
            done = [0, 0]

            def link(ins):
                done[0] += 1
                ins.then_inc(dve_chain, 1)
                hold(dve, dve_chain, done[1] + done[0], passed["dve"])

            def ln1_stats_of(c):
                dve.wait_ge(x_loaded[c], 16)
                if c:
                    dve.wait_ge(ln1_done, c)
                for t in range(QT):
                    nc.vector.bn_stats(stats[:, t, :], x_in[:, QT * c + t, :]).then_inc(dve_chain, 1)
                    done[0] += 1
                dve.wait_ge(dve_chain, done[0])
                for t in range(QT):
                    last = nc.vector.bn_aggr(mv1[:, QT * c + t, :], stats[:, t, :])
                last.then_inc(ln1_stats, 1)

            def ln1_norm(c):
                dve.wait_ge(ln1_rstd, c + 1)
                for t in range(QT * c, QT * (c + 1)):
                    last = nc.vector.tensor_scalar(x_in[:, t, :], x_in[:, t, :], mv1[:, t, 0:1], rstd1[:, t:t + 1],
                                                   ALU.subtract, ALU.mult)
                last.then_inc(ln1_done, 1)

            def split(full, hi, mid, lo, ready):
                link(nc.vector.tensor_copy(hi, full))
                link(nc.vector.tensor_tensor(full, full, hi, ALU.subtract))
                link(nc.vector.tensor_copy(mid, full))
                nc.vector.tensor_tensor(lo, full, mid, ALU.subtract).then_inc(ready, 1)

            def k_split_of(a):
                dve.wait_ge(k_copied, KC * (a + 1))
                split(k_full[:, a, :], *(p[:, a, :] for p in k_part), k_split)

            def q_split_of(c):
                dve.wait_ge(q_copied, 2 * (c + 1))
                split(q_full, *(p[:, :, c * QC:(c + 1) * QC] for p in q_part), q_split)

            ln1_stats_of(0)
            ln1_norm(0)
            k_split_of(0)
            q_split_of(0)
            ln1_stats_of(1)
            ln1_norm(1)
            k_split_of(1)
            q_split_of(1)
            for c in range(2, NC):
                ln1_stats_of(c)
                ln1_norm(c)
                q_split_of(c)
            dve.wait_ge(wv_loaded, 32)
            dve.wait_ge(consts_made, 1)
            for k in range(KT):
                dve.wait_ge(v_filled, k + 1)
                w = KW[k]
                nc.vector.tensor_tensor(v_all[0:w, :, k, :, 0:D],
                                        ps_a[0:w, k % 4, 0:C].rearrange("p (g h d) -> p g h d", g=G, h=HG),
                                        bv_s[0:w, :].rearrange("p (g h d) -> p g h d", g=G, h=HG),
                                        ALU.add).then_inc(v_copied, 1)

            def maxima(s):
                for f, (kind, u, j) in enumerate(A_FILLS):
                    if kind == "shift":
                        continue
                    dve.wait_ge(a_filled, FILLS * s + (f + 1))
                    n = KC * u + j
                    nc.vector.reduce_max(piece_max[:, u, j:j + 1], ps_a[:, f % 4, 0:KPW[j]],
                                         axis=AX.X).then_inc(a_reduced, 1)
                    if (n + 1) % (QT * KC) == 0:
                        h = u // QT
                        dve.wait_ge(a_reduced, HG * QT * KC * s + (n + 1))
                        nc.vector.tensor_reduce(neg_max[:, QT * h:QT * (h + 1)], piece_max[:, QT * h:QT * (h + 1), :],
                                                op=ALU.max, axis=AX.X, negate=True).then_inc(head_max, 1)

            maxima(0)
            with dve.Fori(1, STEPS) as s:
                maxima(s)

            before = done[0]

            def normalize(c, t):
                f = M_AT["att", t]
                dve.wait_ge(m_filled, M_FILLS * c + (f + 1))
                sums = bank_m[f % 2].rearrange("p (h w) -> p h w", w=VW)
                link(nc.vector.reciprocal(rden[:, t, :], sums[:, :, D]))
                nc.vector.tensor_tensor(att[:, t, :].rearrange("p (h d) -> p h d", d=D), sums[:, :, 0:D],
                                        rden[:, t, :].unsqueeze(2).to_broadcast([P, H, D]), ALU.mult).then_inc(att_ready, 1)

            def residual(c, t):
                f = M_AT["proj", t]
                dve.wait_ge(m_filled, M_FILLS * c + (f + 1))
                dve.wait_ge(xb_ready, QT * c + (t + 1))
                if t == 0:
                    wait(dve, stored, 16 * QT * c)
                nc.vector.scalar_tensor_tensor(res[:, t, :], bank_m[f % 2][:, 0:C], tg[:, 0:1], xb[:, t, :],
                                               ALU.mult, ALU.add).then_inc(x1_ready, 1)
                dve.wait_ge(x1_ready, QT * c + (t + 1))
                link(nc.vector.bn_stats(stats[:, t, :], res[:, t, :]))
                nc.vector.bn_aggr(mv2[:, t, :], stats[:, t, :]).then_inc(ln2_stats, 1)

            def route(c):
                f = M_AT["router", 0]
                dve.wait_ge(m_filled, M_FILLS * c + (f + 1))
                logits = bank_m[f % 2][:, 0:16 * QT].rearrange("p (t e) -> p t e", t=QT)
                nc.vector.tensor_reduce(rneg[:, :], logits[:, :, 0:E], op=ALU.max, axis=AX.X,
                                        negate=True).then_inc(rneg_ready, 1)
                hold(dve, router_exp, c + 1, passed["dve"])
                for t in range(QT):
                    link(nc.vector.max(v8[:, t, :], e8[:, t, :]))
                    link(nc.vector.max_index(i8[:, t, :], v8[:, t, :], e8[:, t, :]))
                link(nc.vector.tensor_copy(i2[:, :, :], i8[:, :, 0:2]))
                link(nc.vector.tensor_tensor(s2[:, :], v8[:, :, 0], v8[:, :, 1], ALU.add))
                link(nc.vector.reciprocal(r2[:, :], s2[:, :]))
                link(nc.vector.tensor_scalar(r2[:, :], r2[:, :], tg[:, 1:2], None, ALU.mult))
                link(nc.vector.tensor_tensor(w2[:, :, :], v8[:, :, 0:2], r2[:, :].unsqueeze(2).to_broadcast([P, QT, 2]),
                                             ALU.mult))
                for t in range(QT):
                    for n, half in enumerate((cwa, cwb)):
                        last = nc.vector.tensor_scalar(half[:, t, :], iota[:, :], i2[:, t, n:n + 1], w2[:, t, n:n + 1],
                                                       ALU.is_equal, ALU.mult)
                link(last)
                link(nc.vector.tensor_tensor(cw[:, :, 0:E], cwa[:, :, :], cwb[:, :, :], ALU.add))
                link(nc.vector.tensor_scalar(ez[:, :], ez[:, :], 1.0, None, ALU.add))
                link(nc.vector.reciprocal(s2[:, :], ez[:, :]))
                link(nc.vector.tensor_scalar(cw[:, :, E], s2[:, :], tg[:, 1:2], None, ALU.mult))

            def hidden_of(c, u):
                dve.wait_ge(silu_done, UNITS * c + (u + 1))
                if not (isinstance(c, int) and c == 0 and u < 4):
                    dve.wait_ge(d_filled, QT * PAIRS * c + QT * (u // 2 - 1))
                nc.vector.tensor_tensor(hidden[:, u % 4, :], silu[:, u % 2, :], ps_a[:, 2 * (u % 2) + 1, :],
                                        ALU.mult).then_inc(hidden_ready, 1)

            def combine(c, pair):
                for t in range(QT):
                    d = QT * pair + t
                    dve.wait_ge(d_filled, QT * PAIRS * c + (d + 1))
                    bank = bank_d[d % 2]
                    if pair < E // 2:
                        link(nc.vector.scalar_tensor_tensor(res[:, t, :], bank[:, 0:C], cw[:, t, 2 * pair:2 * pair + 1],
                                                            res[:, t, :], ALU.mult, ALU.add))
                        ins = nc.vector.scalar_tensor_tensor(res[:, t, :], bank[:, C:2 * C],
                                                             cw[:, t, 2 * pair + 1:2 * pair + 2],
                                                             res[:, t, :], ALU.mult, ALU.add)
                    else:
                        ins = nc.vector.scalar_tensor_tensor(res[:, t, :], bank[:, 0:C], cw[:, t, E:E + 1],
                                                             res[:, t, :], ALU.mult, ALU.add)
                    ins.then_inc(combined, 1)
                dve.wait_ge(combined, QT * PAIRS * c + QT * (pair + 1))

            def chunk(c):
                for t in range(QT):
                    normalize(c, t)
                for t in range(QT):
                    residual(c, t)
                dve.wait_ge(ln2_rstd, c + 1)
                for t in range(QT):
                    nc.vector.tensor_scalar(xn2[:, t, :], res[:, t, :], mv2[:, t, 0:1], rstd2[:, t:t + 1],
                                            ALU.subtract, ALU.mult).then_inc(xn2_ready, 1)
                route(c)
                for pair in range(PAIRS):
                    hidden_of(c, 2 * pair)
                    hidden_of(c, 2 * pair + 1)
                    if pair:
                        combine(c, pair - 1)
                combine(c, PAIRS - 1)

            dve.wait_ge(tanh_done, 1)
            chunk(0)
            per = done[0] - before
            with dve.Fori(1, NC) as c:
                done[0], done[1] = 0, c * per + before
                chunk(c)
            assert done[0] == per

        @block.tensor
        def _(pe):
            mm = nc.tensor.matmul

            def project_k(a):
                for j in range(KC):
                    wait(pe, k_copied, KC * (a - 1) + j + 1)
                    for i in range(2):
                        last = mm(ps_a[:, j, 0:KPW[j]], wk_s[:, i, a * P:(a + 1) * P],
                                  ctx_in[:, i, KP0[j]:KP0[j] + KPW[j]], start=(i == 0), stop=(i == 1))
                    last.then_inc(k_filled, 1)

            def transpose_x(c):
                pe.wait_ge(ln1_done, c + 1)
                for a in range(2):
                    wait(pe, xnT_copied, 2 * (c - 1) + a + 1)
                    for t in range(QT):
                        last = mm(ps_b[:, a, t * P:(t + 1) * P], x_in[:, QT * c + t, a * P:(a + 1) * P], ident[:, :],
                                  start=True, stop=True, is_transpose=True)
                    last.then_inc(xnT_filled, 1)

            def project_q(c):
                pe.wait_ge(xnT_copied, 2 * (c + 1))
                for a, bank in enumerate((ps_b[:, 2, :], ps_o[:, :])):
                    wait(pe, q_copied, 2 * (c - 1) + a + 1)
                    for i in range(2):
                        last = mm(bank, wq_s[:, i, a * P:(a + 1) * P], xnT[:, i, :], start=(i == 0), stop=(i == 1))
                    last.then_inc(q_filled, 1)

            pe.wait_ge(wk_loaded, 32)
            pe.wait_ge(ctx_loaded, 16)
            project_k(0)
            pe.wait_ge(consts_made, 1)
            transpose_x(0)
            pe.wait_ge(wq_loaded, 32)
            project_q(0)
            project_k(1)
            for c in range(1, NC):
                transpose_x(c)
                project_q(c)
            pe.wait_ge(wv_loaded, 32)
            pe.wait_ge(k_copied, 2 * KC)
            for k in range(KT):
                wait(pe, v_copied, k - 3)
                for i in range(2):
                    last = mm(ps_a[0:KW[k], k % 4, 0:C], ctx_in[:, i, k * P:k * P + KW[k]], wv_s[:, i, :],
                              start=(i == 0), stop=(i == 1))
                last.then_inc(v_filled, 1)

            def fill_a(s, f, first=False):
                kind, u, j = A_FILLS[f]
                if not (first and f < 4):
                    back, prev = (0, f - 4) if f >= 4 else (1, f - 4 + FILLS)
                    pkind, pu, pj = A_FILLS[prev]
                    if pkind == "score":
                        pe.wait_ge(a_reduced, HG * QT * KC * s + (KC * pu + pj + 1 - back * HG * QT * KC))
                    else:
                        pe.wait_ge(shift_copied, HG * s + (pu + 1 - back * HG))
                if kind == "score":
                    h, t = u // QT, u % QT
                    mm(ps_a[:, f % 4, 0:KPW[j]], queries(s, h, t * P, P, 0, SPLIT), keys(s, h, KP0[j], KPW[j], SPLIT),
                       start=True, stop=True).then_inc(a_filled, 1)
                else:
                    pe.wait_ge(shift_low, HG * s + (u + 1))
                    for t in range(QT):
                        last = mm(ps_a[SPLIT:ROWS, f % 4, t * P:(t + 1) * P], shift[:, QT * u + t, :], ident_b[:, :],
                                  start=True, stop=True)
                    last.then_inc(a_filled, 1)

            def begin_a(s, par):
                pe.wait_ge(q_staged[par], 6 * 16 * (s // 2) + 6 * 16)
                pe.wait_ge(k_staged, 6 * 16 * (s // NC) + 6 * 16)

            def probs_times_v(s, par, k, first=False):
                pe.wait_ge(exp_done, EXPS * s + HG * (k + 1))
                if k == 0:
                    pe.wait_ge(v_staged[par], 16 * (s // 2) + 16)
                    if not first:
                        pe.wait_ge(out_copied, s)
                for h in range(HG):
                    last = mm(ps_o[VW * h:VW * (h + 1), :], v_use[par][0:KW[k], k, h, :],
                              probs[0:KW[k], (k + par) % 2, h, :], start=(k == 0), stop=(k == KT - 1))
                last.then_inc(pv_done, 1)

            def step(s, par, next_a, first=False):
                if next_a:
                    begin_a(s + 1, 1 - par)
                f = 0
                for k in range(KT):
                    share = A_SHARE[k] if next_a else 0
                    for h in range(HG):
                        i = HG * k + h
                        if not (first and i < 3):
                            pe.wait_ge(exp_done, EXPS * s + b_bank_used(i, par))
                        if k == 0:
                            pe.wait_ge(shift_copied, HG * s + (h + 1))
                        mm(ps_b[0:KW[k], b_bank(i, par), :], keys(s, h, k * P, KW[k]), queries(s, h, 0, QC),
                           start=True, stop=True).then_inc(b_filled, 1)
                        n = share * (h + 1) // HG
                        while share > 1 and f < sum(A_SHARE[:k]) + n:
                            fill_a(s + 1, f)
                            f += 1
                    if k:
                        probs_times_v(s, par, k - 1, first)
                    elif not first:
                        probs_times_v(s - 1, 1 - par, KT - 1)
                    if share == 1:
                        fill_a(s + 1, f)
                        f += 1

            pe.wait_ge(v_copied, KT)
            pe.wait_ge(q_copied, 2 * NC)
            begin_a(0, 0)
            for f in range(FILLS):
                fill_a(0, f, first=True)
            step(0, 0, True, first=True)
            with pe.Fori(0, STEPS // 2 - 1) as j:
                step(j * 2 + 1, 1, True)
                step(j * 2 + 2, 0, True)
            step(STEPS - 1, 1, False)
            probs_times_v(STEPS - 1, 1, KT - 1)

            def fill_m(c, f):
                kind, t = M_ORDER[f]
                back, prev = (0, f - 2) if f >= 2 else (1, max(g for g in range(M_FILLS) if g % 2 == f % 2))
                pkind, pt = M_ORDER[prev]
                gone, each = {"att": (att_ready, QT), "attT": (attT_ready, QT), "proj": (x1_ready, QT),
                              "xn2T": (xn2T_ready, 2), "router": (router_exp, 1)}[pkind]
                wait(pe, gone, each * c + (pt + 1 - back * each))
                bank = bank_m[f % 2]
                if kind == "att":
                    for g in range(G):
                        last = mm(bank[:, g * P:(g + 1) * P], outT[:, g, t * P:(t + 1) * P], ident[:, :],
                                  start=True, stop=True, is_transpose=True)
                elif kind == "attT":
                    pe.wait_ge(att_ready, QT * c + (t + 1))
                    for a in range(2):
                        last = mm(bank[:, a * P:(a + 1) * P], att[:, t, a * P:(a + 1) * P], ident[:, :],
                                  start=True, stop=True, is_transpose=True)
                elif kind == "proj":
                    pe.wait_ge(attT_ready, QT * c + (t + 1))
                    for a in range(2):
                        last = mm(bank[:, 0:C], attT[:, a, t * P:(t + 1) * P], wo_s[:, a, :],
                                  start=(a == 0), stop=(a == 1))
                elif kind == "xn2T":
                    pe.wait_ge(xn2_ready, QT * c + QT)
                    for i in range(QT):
                        last = mm(bank[:, i * P:(i + 1) * P], xn2[:, i, t * P:(t + 1) * P], ident[:, :],
                                  start=True, stop=True, is_transpose=True)
                else:
                    pe.wait_ge(xn2T_ready, 2 * c + 2)
                    for i in range(QT):
                        for a in range(2):
                            last = mm(bank[:, 16 * i:16 * i + E + 1], xn2T[:, a, i * P:(i + 1) * P], rt_w[:, a, :],
                                      start=(a == 0), stop=(a == 1))
                last.then_inc(m_filled, 1)

            def gate_up(c, u):
                if not (isinstance(c, int) and c == 0 and u < 2):
                    pe.wait_ge(hidden_ready, UNITS * c + (u - 1))
                for n in range(2):
                    for a in range(2):
                        if u < E:
                            w = gu_w[:, a, 2 * I * u + I * n:2 * I * u + I * (n + 1)]
                        else:
                            w = (sg_w, su_w)[n][:, a, P * (u - E):P * (u - E + 1)]
                        last = mm(ps_a[:, 2 * (u % 2) + n, :], w, xn2T[:, a, :], start=(a == 0), stop=(a == 1))
                last.then_inc(gu_filled, 1)

            def down(c, pair):
                pe.wait_ge(hidden_ready, UNITS * c + 2 * (pair + 1))
                for t in range(QT):
                    d = QT * pair + t
                    if not (isinstance(c, int) and c == 0 and d < 2):
                        pe.wait_ge(combined, QT * PAIRS * c + (d - 1))
                    for n in range(2):
                        u = 2 * pair + n
                        h = hidden[:, u % 4, t * P:(t + 1) * P]
                        if u < E:
                            last = mm(bank_d[d % 2][:, n * C:(n + 1) * C], h, dw_w[:, u, :], start=True, stop=True)
                        else:
                            last = mm(bank_d[d % 2][:, 0:C], h, sd_w[:, u - E, :], start=(n == 0), stop=(n == 1))
                    last.then_inc(d_filled, 1)

            def chunk(c):
                pe.wait_ge(outT_loaded, 16 * c + 16)
                for f in range(M_FILLS):
                    fill_m(c, f)
                for pair in range(PAIRS):
                    gate_up(c, 2 * pair)
                    gate_up(c, 2 * pair + 1)
                    if pair:
                        down(c, pair - 1)
                down(c, PAIRS - 1)

            pe.wait_ge(out_copied, STEPS)
            pe.wait_ge(a_reduced, HG * QT * KC * STEPS)
            pe.wait_ge(wo_loaded, 16 * 5)
            pe.wait_ge(ffw_loaded, 16 * 5)
            chunk(0)
            with pe.Fori(1, NC) as c:
                chunk(c)


M_ORDER = [("att", 0), ("att", 1), ("attT", 0), ("att", 2), ("attT", 1), ("proj", 0), ("att", 3), ("attT", 2),
           ("proj", 1), ("attT", 3), ("proj", 2), ("proj", 3), ("xn2T", 0), ("xn2T", 1), ("router", 0)]
M_FILLS = len(M_ORDER)
M_AT = {what: f for f, what in enumerate(M_ORDER)}


def kernel(x, ctx_1024, g_xattn, g_ffn, L0_xattn_Wq, L0_xattn_bq, L0_xattn_Wk, L0_xattn_bk, L0_xattn_Wv,
           L0_xattn_bv, L0_xattn_Wo, L0_xattn_bo, L0_ffn_router_weight, L0_ffn_gate_up_proj, L0_ffn_down_proj,
           L0_ffn_shared_gate_w, L0_ffn_shared_up_w, L0_ffn_shared_down_w, L0_ffn_shared_expert_gate_w):
    import numpy as np
    import concourse.bacc as bacc
    from concourse.bass_utils import run_bass_kernel_spmd

    def cols(w):
        w = np.asarray(w)
        return np.ascontiguousarray(w.T.reshape(-1, P, w.shape[0]).transpose(1, 0, 2))

    order = np.arange(C).reshape(2, 2, HG, D).transpose(0, 1, 3, 2).reshape(-1)
    arrays = {
        "x": np.ascontiguousarray(np.asarray(x)[0]),
        "ctxT": np.ascontiguousarray(np.asarray(ctx_1024)[0].T.reshape(2, P, NK).transpose(1, 0, 2)),
        "wq": cols(np.asarray(L0_xattn_Wq)[order]), "wk": cols(np.asarray(L0_xattn_Wk)[order]),
        "wv": cols(L0_xattn_Wv), "wo": cols(L0_xattn_Wo),
        "bq": np.ascontiguousarray(np.asarray(L0_xattn_bq)[order].reshape(2, P).T),
        "bk": np.ascontiguousarray(np.asarray(L0_xattn_bk)[order].reshape(2, P).T),
        "bv": np.asarray(L0_xattn_bv), "bo": np.asarray(L0_xattn_bo),
        "g_x": np.asarray(g_xattn), "g_f": np.asarray(g_ffn),
        "router": cols(np.concatenate([np.asarray(L0_ffn_router_weight), np.asarray(L0_ffn_shared_expert_gate_w)])),
        "gu": cols(np.asarray(L0_ffn_gate_up_proj).reshape(E * 2 * I, C)),
        "dw": np.ascontiguousarray(np.asarray(L0_ffn_down_proj).transpose(2, 0, 1)),
        "sg": cols(L0_ffn_shared_gate_w), "su": cols(L0_ffn_shared_up_w), "sd": cols(L0_ffn_shared_down_w),
    }
    nc = bacc.Bacc("TRN2", target_bir_lowering=False, num_devices=1)
    aps = [nc.dram_tensor(f"in_{n}", a.shape, mybir.dt.from_np(a.dtype), kind="ExternalInput").ap()
           for n, a in arrays.items()]
    result = nc.dram_tensor("result", (NT, C), F32, kind="ExternalOutput").ap()
    flamingo_block(nc, *aps, result)
    got = run_bass_kernel_spmd(nc, [{f"in_{n}": a for n, a in arrays.items()}], core_ids=[0])
    return got.results[0]["result"].reshape(1, NT, C)
```

```python
from contextlib import ExitStack

import concourse.bass as bass
from concourse import mybir

F32 = mybir.dt.float32
F32R = mybir.dt.float32r
BF16 = mybir.dt.bfloat16
U32 = mybir.dt.uint32
ALU = mybir.AluOpType
ACT = mybir.ActivationFunctionType
AX = mybir.AxisListType

P = 128
C = 256
NT = 2048
NK = 1601
H, D = 16, 16
HG = 4
G = H // HG
QC = 512
NC = NT // QC
QT = QC // P
STEPS = G * NC
KT = -(-NK // P)
KW = [min(P, NK - P * k) for k in range(KT)]
KC = 4
KP0 = [401 * j - max(0, j - 1) for j in range(KC)]
KPW = [401] + [400] * (KC - 1)
SPLIT = 6 * D
ROWS = SPLIT + 2
VW = 32
SCALE = D ** -0.5
EPS = 1e-5
E, I, SI = 8, 128, 512
UNITS = E + SI // P
PAIRS = UNITS // 2

FILLS = QT * HG * KC + HG
EXPS = KT * HG
Q_PARTS = [0, 0, 0, 1, 1, 2]
K_PARTS = [0, 1, 2, 0, 1, 0]


def pass_a_fills():
    out, due = [], []
    for i in range(HG * QT * KC):
        out.append(("score", i // KC, i % KC))
        if (i + 1) % (QT * KC) == 0:
            due.append((i + 4, i // (QT * KC)))
        if due and i == due[0][0]:
            out.append(("shift", due.pop(0)[1], 0))
    return out + [("shift", h, 0) for _, h in due]


A_FILLS = pass_a_fills()
A_SHARE = [6, 6, 5, 6, 6, 5, 6, 6, 5, 6, 5, 5, 1]
assert sum(A_SHARE) == FILLS == len(A_FILLS)
SHIFT_AT = [A_FILLS.index(("shift", h, 0)) for h in range(HG)]



PRO_FIRST = [("k", j) for j in range(KC)] + [("x", 0), ("x", 1), ("q", 0), ("q", 1)]
PRO_LATER = ([("x", 2), ("x", 3), ("q", 2), ("q", 3)] + [("v", k) for k in range(KT)]
             + [(kind, 2 * c + a) for c in range(2, NC) for kind in "xq" for a in range(2)]
             + [("k", KC + j) for j in range(KC)])
PRO = PRO_FIRST + PRO_LATER
PRO_AT = {what: n for n, what in enumerate(PRO)}


def first_pass_a():
    out, later, due = [], list(PRO_LATER), []
    for f in range(FILLS):
        out.append(("a", f))
        kind, u, j = A_FILLS[f]
        if kind == "score" and (u + 1) % QT == 0 and j == KC - 1:
            out.append(("shift", u // QT))
        if f % 2 and later:
            what = later.pop(0)
            out.append(("p", what))
            if what[0] == "q" and what[1] % 2 or what == PRO_LATER[-1]:
                due.append((f + 4, what))
        if due and f >= due[0][0]:
            out.append(("mid", due.pop(0)[1]))
    return out + [("p", what) for what in later] + [("mid", what) for _, what in due]


FIRST_A = first_pass_a()
assert sum(kind == "p" for kind, _ in FIRST_A) == len(PRO_LATER)

M_ORDER = [("att", 0), ("att", 1), ("attT", 0), ("att", 2), ("attT", 1), ("proj", 0), ("att", 3), ("attT", 2),
           ("proj", 1), ("attT", 3), ("proj", 2), ("proj", 3), ("xn2T", 0), ("xn2T", 1), ("router", 0)]
M_FILLS = len(M_ORDER)
M_AT = {what: f for f, what in enumerate(M_ORDER)}
M_AT_PLACE = [[0, 1, None, 2], [3, None, 4, 5], [6, 7, None, 8], [9, None, 10, None], [11, None, None, None],
              [None] * QT]
LAST_SHARE = [[k] if k < M_AT["xn2T", 0] else [] for k in range(KT)]
LAST_FILLS = range(M_AT["xn2T", 0])
W_SPLITS = ["gu0", "dw0", "gu1", "dw1", "sg", "su", "sd"]


def wait(eng, sem, value):
    if not (isinstance(value, int) and value <= 0):
        eng.wait_ge(sem, value)


def hold(eng, sem, value, passed):
    eng.wait_ge(sem, value)
    eng.sem_inc(passed, 1)


def flamingo_block(nc, x, ctxT, wq, wk, wv, wo, bq, bk, bv, bo, g_x, g_f, router, gu, dw, sg, su, sd, out):
    with ExitStack() as ctx:
        def sb(name, shape, dt=F32):
            return ctx.enter_context(nc.sbuf_tensor(name, shape, dt))

        def sem(name):
            return ctx.enter_context(nc.semaphore(name))

        SPLITW = 3 * 2 * NT + 3 * 2 * NK
        VG = KT * HG * VW
        KSW = HG * NK
        TW = QT * C
        sizes = {"parts": 2 * SPLITW, "v_all": 4 * G * VG, "v0": 4 * VG, "v1": 4 * VG, "k_stack": 2 * 2 * KSW,
                 "q_stack": 2 * NC * HG * QC, "probs": 4 * 2 * HG * QC, "big": 4 * STEPS * QC,
                 "temp": 4 * (2 * NK + 2 * QC), "xnT": 4 * 2 * QC}
        sizes = {n: -(-b // 32) * 32 + 32 * (n == "parts") * 5 for n, b in sizes.items()}
        base = -(-nc.sbuf_base // 32) * 32
        slab = sb("slab", [P, sum(sizes.values()) // 4])
        region = {}
        for n, b in sizes.items():
            region[n], base = [base, base + b], base + b

        def at(where, name, shape, dt=F32):
            width = 4 if dt in (F32, F32R) else 2
            for n in shape[1:]:
                width *= n
            lo, hi = region[where]
            at_ = used.get(where, lo)
            used[where] = -(-(at_ + width) // 32) * 32
            assert at_ + width <= hi, (name, at_ + width - hi)
            return nc.alloc_sbuf_tensor_at(name, shape, dt, offset=at_)

        used = {}
        q_part = [at("parts", f"q_part{i}", [P, 2, NT], BF16) for i in range(3)]
        k_part = [at("parts", f"k_part{i}", [P, 2, NK], BF16) for i in range(3)]
        v_mem = at("v_all", "v_all", [P, G * VG])
        v_all = v_mem[:, :].rearrange("p (g k h w) -> p g k h w", g=G, k=KT, h=HG)
        v_grp = [at(f"v{i}", f"v_group{i}", [P, VG]) for i in range(2)]
        v_use = [v[:, :].rearrange("p (k h w) -> p k h w", k=KT, h=HG) for v in v_grp]
        k_stack = at("k_stack", "k_stack", [P, 2 * KSW], BF16)
        q_stack = at("q_stack", "q_stack", [P, NC * HG * QC], BF16)
        probs = at("probs", "probs", [P, 2, HG, QC])
        big = at("big", "attention_out", [P, STEPS * QC])
        k_full = at("temp", "k_full", [P, 2, NK])
        q_full = at("temp", "q_full", [P, 2, QC])
        xnT = at("xnT", "xnT", [P, 2, QC])
        used = {}
        x_in = at("big", "x_in", [P, 16, C])
        ctx_in = at("big", "ctx_in", [P, 2, NK])
        w_raw = {"gu0": at("parts", "gu0", [P, 2, E * I]), "gu1": at("parts", "gu1", [P, 2, E * I]),
                 "dw0": at("parts", "dw0", [P, E // 2, C]), "dw1": at("parts", "dw1", [P, E // 2, C]),
                 "sg": at("parts", "sg", [P, 2, SI]), "su": at("parts", "su", [P, 2, SI]),
                 "sd": at("parts", "sd", [P, SI // P, C])}
        used = {}
        w_lo = {n: at("parts", n + "_lo", list(w_raw[n].shape), F32R)
                for n in ("gu0", "gu1", "dw0", "dw1", "sg", "su", "sd")}
        where = {"gu0": "k_stack", "dw0": "k_stack", "gu1": "q_stack", "dw1": "q_stack", 
                 "sg": "v0", "su": "xnT", "sd": "parts"}
        w_hi = {n: at(where[n], n + "_hi", list(w_raw[n].shape), F32R) for n in where}
        xb, x1, res, xn2, att = (at("v_all", n, [P, QT, C]) for n in ("x_again", "x1", "res", "xn2", "att"))
        attT = at("v_all", "attT", [P, 2, QC])
        outT = at("temp", "outT", [P, G, QC])
        xn2T_hi, xn2T_lo = (at("temp", n, [P, 2, QC], F32R) for n in ("xn2T_hi", "xn2T_lo"))
        silu = at("v1", "silu", [P, 2, QC])
        hid = [at(f"v{i}", f"hidden{i}", [P, QC]) for i in range(2)]
        hid_hi, hid_lo = (at("probs", n, [P, 4, QC], F32R) for n in ("hidden_hi", "hidden_lo"))

        wq_s, wk_s, wv_s, wo_s = (sb(n, [P, 2, C]) for n in ("wq", "wk", "wv", "wo"))
        bq_s, bk_s = sb("bq", [P, 2]), sb("bk", [P, 2])
        bv_s, bo_s = sb("bv", [P, C]), sb("bo", [P, C])
        rt_w = sb("router", [P, 2, E + 2])
        rt_hi, rt_lo = sb("router_hi", [P, 2, E + 2], F32R), sb("router_lo", [P, 2, E + 2], F32R)
        gates = sb("gates", [P, 2])
        tg = sb("tanh_gates", [P, 2])
        ident = sb("ident", [P, P])
        ident_b = sb("ident_b", [P, P], BF16)
        mhalf = sb("minus_half", [P, QT])
        iota = sb("iota", [P, E])
        stats = sb("stats", [P, QT, 6])
        mv1 = sb("mean_var1", [P, 16, 2])
        rstd1 = sb("rstd1", [P, 16])
        piece_max = sb("piece_max", [P, HG * QT, KC])
        neg_max = sb("neg_max", [P, HG * QT])
        shift = sb("shift_parts", [P, HG * QT, 2], BF16)
        rden = sb("rden", [P, QT, H])
        mv2 = sb("mean_var2", [P, QT, 2])
        rstd2 = sb("rstd2", [P, QT])
        rneg = sb("router_neg_max", [P, QT])
        e8 = sb("router_exp", [P, QT, E])
        ez = sb("gate_exp", [P, QT])
        v8 = sb("top_values", [P, QT, 8])
        i8 = sb("top_index", [P, QT, 8], U32)
        i2 = sb("top2_index", [P, QT, 2])
        s2 = sb("top2_sum", [P, QT])
        r2 = sb("top2_scale", [P, QT])
        w2 = sb("top2_weight", [P, QT, 2])
        cwa, cwb = sb("weights_first", [P, QT, E]), sb("weights_second", [P, QT, E])
        cw = sb("weights", [P, QT, E + 1])

        ps_a = ctx.enter_context(nc.psum_tensor("ps_a", [P, 4, 512], F32))
        ps_b = ctx.enter_context(nc.psum_tensor("ps_b", [P, 3, 512], F32))
        ps_o = ctx.enter_context(nc.psum_tensor("ps_o", [P, 512], F32))
        bank_p = [ps_b[:, 0, :], ps_b[:, 1, :], ps_b[:, 2, :], ps_o[:, :]]

        def bank_m(c, f):
            return ps_a[:, 2 + f % 2, :] if isinstance(c, int) and c == 0 else (ps_b[:, 2, :], ps_o[:, :])[f % 2]

        bank_d = [ps_b[:, 0, :], ps_b[:, 1, :]]

        x_loaded = [sem(f"x_loaded{c}") for c in range(NC)]
        ctx_loaded = [sem(f"ctx_loaded{j}") for j in range(KC)]
        wk_loaded, wq_loaded = sem("wk_loaded"), sem("wq_loaded")
        wv_loaded, wo_loaded = sem("wv_loaded"), sem("wo_loaded")
        consts_made, pool_chain, dve_chain = sem("consts_made"), sem("pool_chain"), sem("dve_chain")
        ln1_stats, ln1_rstd, ln1_done = sem("ln1_stats"), sem("ln1_rstd"), sem("ln1_done")
        xnT_copied, v_ones, high_off, mid_done = sem("xnT_copied"), sem("v_ones"), sem("high_off"), sem("mid_done")
        key_ones, w_high, w_low, h_ready = sem("key_ones"), sem("w_high"), sem("w_low"), sem("h_ready")
        p_filled, k_copied, k_split = sem("p_filled"), sem("k_copied"), [sem("k_split0"), sem("k_split1")]
        q_copied, q_split = sem("q_copied"), sem("q_split")
        v_copied = sem("v_copied")
        k_staged, q_staged, v_staged = sem("k_staged"), [sem("q_staged0"), sem("q_staged1")], [sem("v_staged0"), sem("v_staged1")]
        a_filled, a_reduced, head_max = sem("a_filled"), sem("a_reduced"), sem("head_max")
        shift_high, shift_low, shift_copied = sem("shift_high"), sem("shift_low"), sem("shift_copied")
        b_filled, exp_done, pv_done, out_copied = sem("b_filled"), sem("exp_done"), sem("pv_done"), sem("out_copied")
        tanh_done, bo_scaled = sem("tanh_done"), sem("bo_scaled")
        ffw_loaded, outT_loaded, xb_loaded, xb_ready = sem("ffw_loaded"), sem("outT_loaded"), sem("xb_loaded"), sem("xb_ready")
        m_filled, att_ready, attT_ready, x1_ready = sem("m_filled"), sem("att_ready"), sem("attT_ready"), sem("x1_ready")
        ln2_stats, ln2_eps, ln2_rstd, xn2_ready = sem("ln2_stats"), sem("ln2_eps"), sem("ln2_rstd"), sem("xn2_ready")
        xn2T_high, rt_split = sem("xn2T_high"), sem("rt_split")
        xn2T_ready, rneg_ready, router_exp = sem("xn2T_ready"), sem("rneg_ready"), sem("router_exp")
        gu_filled, silu_done = sem("gu_filled"), sem("silu_done")
        hidden_high, hidden_low = sem("hidden_high"), sem("hidden_low")
        passed = {"pool": sem("pool_passed"), "dve": sem("dve_passed")}
        d_filled, combined, stored = sem("d_filled"), sem("combined"), [sem(f"stored{t}") for t in range(QT)]

        def keys(s, h, k0, n, rows=ROWS):
            at = (s // NC) % 2 * KSW + (h * NK + k0)
            return k_stack[0:rows, at:at + n] if isinstance(at, int) else k_stack[0:rows, bass.ds(at, n)]

        def queries(s, h, q0, n, lo=0, hi=ROWS):
            at = (s % NC) * (HG * QC) + (h * QC + q0)
            return q_stack[lo:hi, at:at + n] if isinstance(at, int) else q_stack[lo:hi, bass.ds(at, n)]

        def out_at(s):
            return big[:, s * QC:(s + 1) * QC] if isinstance(s, int) else big[:, bass.ds(s * QC, QC)]

        def b_bank(i, par):
            return (i + par) % 3

        def b_bank_used(i, par):
            if i >= 3:
                return i - 2
            last = max(j for j in range(EXPS) if b_bank(j, 1 - par) == b_bank(i, par))
            return last + 1 - EXPS

        def consumer(what):
            kind, n = what
            return {"k": k_copied, "x": xnT_copied, "q": q_copied, "v": v_copied}[kind], n + 1

        def parts_of(what):
            kind, n = what
            if kind == "q":
                c = n // 2
                return q_full[:, :, :], *(p[:, :, c * QC:(c + 1) * QC] for p in q_part)
            a = n // KC
            return k_full[:, a, :], *(p[:, a, :] for p in k_part)

        block = ctx.enter_context(nc.Block())

        @block.sync
        def _(sp):
            x_chunks = x.rearrange("(c t p) n -> c p t n", c=NC, p=P)
            sp.dma_start(wk_s[:, :, :], wk).then_inc(wk_loaded, 16)
            sp.dma_start(bk_s[:, :], bk).then_inc(wk_loaded, 16)
            sp.dma_start(x_in[:, 0:QT, :], x_chunks[0]).then_inc(x_loaded[0], 16)
            for j in range(KC):
                sp.dma_start(ctx_in[:, :, KP0[j]:KP0[j] + KPW[j]],
                             ctxT[:, :, KP0[j]:KP0[j] + KPW[j]]).then_inc(ctx_loaded[j], 16)
            sp.dma_start(wq_s[:, :, :], wq).then_inc(wq_loaded, 16)
            sp.dma_start(bq_s[:, :], bq).then_inc(wq_loaded, 16)
            for c in range(1, NC):
                sp.dma_start(x_in[:, QT * c:QT * (c + 1), :], x_chunks[c]).then_inc(x_loaded[c], 16)
            sp.dma_start(wv_s[:, :, :], wv).then_inc(wv_loaded, 16)
            sp.dma_start(bv_s[:, :], bv.partition_broadcast(P)).then_inc(wv_loaded, 16)

            def stage_k(g):
                wait(sp, k_staged, 6 * 16 * g)
                sp.wait_ge(k_split[g // 2], 1)
                for r, part in enumerate(K_PARTS):
                    src = k_part[part][64 * (g % 2):64 * (g % 2) + 64, g // 2, :]
                    dst = k_stack[D * r:D * (r + 1), g % 2 * KSW:(g % 2 + 1) * KSW]
                    sp.dma_start(dst.rearrange("p (h n) -> p h n", h=HG), src).then_inc(k_staged, 16)

            def stage_q(s):
                g, c = s // NC, s % NC
                wait(sp, q_staged[s % 2], 6 * 16 * (s // 2))
                sp.wait_ge(q_split, c + 1)
                for r, part in enumerate(Q_PARTS):
                    src = q_part[part][64 * (g % 2):64 * (g % 2) + 64, g // 2, c * QC:(c + 1) * QC]
                    dst = q_stack[D * r:D * (r + 1), c * HG * QC:(c + 1) * HG * QC]
                    sp.dma_start(dst.rearrange("p (h n) -> p h n", h=HG), src).then_inc(q_staged[s % 2], 16)

            def stage_v(s):
                g = s // NC
                wait(sp, v_staged[s % 2], 16 * (s // 2))
                sp.dma_start(v_grp[s % 2][:, :], v_mem[:, g * VG:(g + 1) * VG]).then_inc(v_staged[s % 2], 16)

            stage_k(0)
            stage_q(0)
            sp.dma_start(wo_s[:, :, :], wo).then_inc(wo_loaded, 16)
            sp.dma_start(bo_s[:, :], bo.partition_broadcast(P)).then_inc(wo_loaded, 16)
            sp.wait_ge(consts_made, 1)
            sp.dma_start(rt_w[:, :, 0:E + 1], router).then_inc(wo_loaded, 16)
            sp.dma_start(gates[:, 0:1], g_x.partition_broadcast(P)).then_inc(wo_loaded, 16)
            sp.dma_start(gates[:, 1:2], g_f.partition_broadcast(P)).then_inc(wo_loaded, 16)
            stage_k(1)
            stage_q(1)
            sp.wait_ge(v_copied, KT)
            stage_v(0)
            stage_v(1)
            for s in range(2, NC):
                stage_q(s)
            for t in range(STEPS - 2):
                sp.wait_ge(pv_done, KT * (t + 1))
                stage_v(t + 2)
                if t + NC < STEPS:
                    stage_q(t + NC)
                if t + 1 in (NC, 2 * NC):
                    stage_k((t + 1) // NC + 1)
                if t + NC == STEPS - 1:
                    sp.wait_ge(q_staged[0], 6 * 16 * STEPS // 2)
                    sp.wait_ge(q_staged[1], 6 * 16 * STEPS // 2)
                    sp.wait_ge(k_staged, 6 * 16 * G)
                    for dst, src in (("gu0", gu[:, :, 0:E * I]), ("gu1", gu[:, :, E * I:]), ("dw0", dw[:, 0:E // 2, :]),
                                     ("dw1", dw[:, E // 2:, :]), ("sg", sg), ("su", su), ("sd", sd)):
                        sp.dma_start(w_raw[dst][:, :, :], src).then_inc(ffw_loaded, 16)

            x_c = x.rearrange("(c t p) n -> c p t n", c=NC, p=P)
            o_c = out.rearrange("(c t p) n -> c t p n", c=NC, p=P)
            big_c = big[:, :].rearrange("p (g c n) -> p g c n", g=G, c=NC)

            def load_chunk(c):
                wait(sp, x1_ready, QT * c)
                sp.dma_start(xb[:, :, :], x_c[c]).then_inc(xb_loaded, 16)
                sp.wait_ge(out_copied, STEPS - NC + c + 1)
                wait(sp, att_ready, QT * c)
                sp.dma_start(outT[:, :, :], big_c[:, :, c, :]).then_inc(outT_loaded, 16)

            def store_chunk(c):
                for t in range(QT):
                    sp.wait_ge(combined, c * QT * PAIRS + QT * (PAIRS - 1) + t + 1)
                    sp.dma_start(o_c[c, t], res[:, t, :]).then_inc(stored[t], 16)

            sp.wait_ge(v_staged[0], 16 * STEPS // 2)
            sp.wait_ge(v_staged[1], 16 * STEPS // 2)
            load_chunk(0)
            load_chunk(1)
            for c in range(NC):
                if c + 2 < NC:
                    load_chunk(c + 2)
                store_chunk(c)
            for t in range(QT):
                sp.wait_ge(stored[t], 16 * NC)

        @block.gpsimd
        def _(pool):
            done = [0]

            def link(ins):
                done[0] += 1
                ins.then_inc(pool_chain, 1)
                pool.wait_ge(pool_chain, done[0])

            link(nc.gpsimd.memset(ident[:, :], 0.0))
            link(nc.gpsimd.affine_select(out=ident[:, :], in_=ident[:, :], compare_op=ALU.not_equal, fill=1.0,
                                         base=0, pattern=[[-1, P]], channel_multiplier=1))
            link(nc.gpsimd.tensor_copy(ident_b[:, :], ident[:, :]))
            link(nc.gpsimd.memset(mhalf[:, :], -0.5))
            nc.gpsimd.memset(rt_w[:, :, :], 0.0).then_inc(consts_made, 1)
            pool.wait_ge(consts_made, 1)

            def rstd1_of(c):
                sl = slice(QT * c, QT * (c + 1))
                pool.wait_ge(ln1_stats, c + 1)
                link(nc.gpsimd.tensor_scalar(rstd1[:, sl], mv1[:, sl, 1], EPS, None, ALU.add))
                nc.gpsimd.tensor_tensor(rstd1[:, sl], rstd1[:, sl], mhalf[:, :], ALU.pow).then_inc(ln1_rstd, 1)
                pool.wait_ge(ln1_rstd, c + 1)

            rstd1_of(0)
            blocks = v_mem[:, :].rearrange("p (a w) -> p a w", w=VW)
            link(nc.gpsimd.memset(blocks[:, :, D:VW], 0.0))
            link(nc.gpsimd.memset(v_all[:, :, KT - 1, :, :], 0.0))
            nc.gpsimd.memset(blocks[:, :, D:D + 1], 1.0).then_inc(v_ones, 1)
            pool.wait_ge(v_ones, 1)
            for c in range(1, NC):
                rstd1_of(c)
            nc.gpsimd.memset(k_stack[SPLIT:ROWS, :], 1.0).then_inc(key_ones, 1)
            pool.wait_ge(key_ones, 1)
            for e in range(E):
                link(nc.gpsimd.memset(iota[:, e:e + 1], float(e)))

            def shift_of(s, h):
                u = slice(QT * h, QT * (h + 1))
                hold(pool, head_max, HG * s + (h + 1), passed["pool"])
                nc.gpsimd.tensor_copy(shift[:, u, 0], neg_max[:, u]).then_inc(shift_high, 1)
                pool.wait_ge(shift_high, HG * s + (h + 1))
                nc.gpsimd.tensor_tensor(shift[:, u, 1], neg_max[:, u], shift[:, u, 0],
                                        ALU.subtract).then_inc(shift_low, 1)

            n_split = 0
            for kind, what in FIRST_A:
                if kind == "shift":
                    shift_of(0, what)
                elif kind == "p" and (what[0] == "q" and what[1] % 2 or what == PRO_LATER[-1]):
                    full, hi, _, _ = parts_of(what)
                    pool.wait_ge(*consumer(what))
                    nc.gpsimd.tensor_tensor(full, full, hi, ALU.subtract).then_inc(high_off, 1)
                elif kind == "mid":
                    full, _, mid, lo = parts_of(what)
                    n_split += 1
                    pool.wait_ge(mid_done, n_split)
                    nc.gpsimd.tensor_tensor(lo, full, mid, ALU.subtract).then_inc(
                        q_split if what[0] == "q" else k_split[1], 1)
            with pool.Fori(1, STEPS) as s:
                for h in range(HG):
                    shift_of(s, h)

            pool.wait_ge(tanh_done, 1)
            nc.gpsimd.tensor_scalar(bo_s[:, :], bo_s[:, :], tg[:, 0:1], None, ALU.mult).then_inc(bo_scaled, 1)
            pool.wait_ge(bo_scaled, 1)

            def residual_input(c):
                pool.wait_ge(xb_loaded, 16 * c + 16)
                for t in range(QT):
                    nc.gpsimd.tensor_tensor(xb[:, t, :], xb[:, t, :], bo_s[:, :], ALU.add).then_inc(xb_ready, 1)

            def rstd2_of(c):
                hold(pool, ln2_stats, QT * c + QT, passed["pool"])
                nc.gpsimd.tensor_scalar(rstd2[:, :], mv2[:, :, 1], EPS, None, ALU.add).then_inc(ln2_eps, 1)
                pool.wait_ge(ln2_eps, c + 1)
                nc.gpsimd.tensor_tensor(rstd2[:, :], rstd2[:, :], mhalf[:, :], ALU.pow).then_inc(ln2_rstd, 1)

            def low_weights(n):
                pool.wait_ge(w_high, n + 1)
                w = W_SPLITS[n]
                nc.gpsimd.tensor_tensor(w_lo[w][:, :, :], w_raw[w][:, :, :], w_hi[w][:, :, :].bitcast(F32),
                                        ALU.subtract).then_inc(w_low, 1)

            def hidden_low_of(c, u):
                pool.wait_ge(hidden_high, UNITS * c + (u + 1))
                nc.gpsimd.tensor_tensor(hid_lo[:, u % 4, :], hid[u % 2][:, :], hid_hi[:, u % 4, :].bitcast(F32),
                                        ALU.subtract).then_inc(hidden_low, 1)

            residual_input(0)
            low_weights(0)
            low_weights(1)
            rstd2_of(0)
            for n in range(2, len(W_SPLITS)):
                low_weights(n)

            def experts(c, next_m=True):
                if next_m:
                    residual_input(c + 1)
                for u in range(UNITS):
                    hidden_low_of(c, u)
                    if next_m and u == UNITS - 4:
                        rstd2_of(c + 1)

            experts(0)
            with pool.Fori(1, NC - 1) as c:
                experts(c)
            experts(NC - 1, False)

        @block.scalar
        def _(act):
            def copy_p(what, split):
                kind, n = what
                act.wait_ge(p_filled, PRO_AT[what] + 1)
                bank = bank_p[PRO_AT[what] % 4]
                if kind == "x":
                    wait(act, p_filled, PRO_AT.get(("q", n // 2 * 2 - 1), -1) + 1)
                    nc.scalar.copy(xnT[:, n % 2, :], bank).then_inc(xnT_copied, 1)
                    return
                if kind == "k":
                    a, j = n // KC, n % KC
                    cols = slice(KP0[j], KP0[j] + KPW[j])
                    full, hi, bias, bank, sem_ = k_full[:, a, cols], k_part[0][:, a, cols], bk_s[:, a:a + 1], bank[:, 0:KPW[j]], k_copied
                else:
                    c, a = n // 2, n % 2
                    wait(act, q_split, c)
                    full, hi, bias, sem_ = q_full[:, a, :], q_part[0][:, a, c * QC:(c + 1) * QC], bq_s[:, a:a + 1], q_copied
                ins = nc.scalar.activation(full, bank, ACT.Identity, bias=bias)
                if split:
                    ins = nc.scalar.activation(hi, bank, ACT.Identity, bias=bias)
                ins.then_inc(sem_, 1)

            act.wait_ge(wk_loaded, 32)
            act.wait_ge(wq_loaded, 32)
            for what in PRO_FIRST:
                copy_p(what, False)

            def copy_shift(s, h):
                f = SHIFT_AT[h]
                act.wait_ge(a_filled, FILLS * s + (f + 1))
                nc.scalar.copy(queries(s, h, 0, QC, SPLIT, ROWS), ps_a[SPLIT:ROWS, f % 4, :]).then_inc(shift_copied, 1)

            n_split = 0
            for kind, what in FIRST_A:
                if kind == "a" and A_FILLS[what][0] == "shift":
                    copy_shift(0, A_FILLS[what][1])
                elif kind == "p" and what[0] != "v":
                    copy_p(what, True)
                elif kind == "mid":
                    n_split += 1
                    act.wait_ge(high_off, n_split)
                    full, _, mid, _ = parts_of(what)
                    nc.scalar.copy(mid, full).then_inc(mid_done, 1)
            act.wait_ge(wo_loaded, 16 * 5)
            nc.scalar.activation(tg[:, :], gates[:, :], ACT.Tanh).then_inc(tanh_done, 1)

            def copy_out(s):
                act.wait_ge(pv_done, KT * s + KT)
                nc.scalar.copy(out_at(s), ps_o[:, :]).then_inc(out_copied, 1)

            def copy_m(c, f):
                kind, t = M_ORDER[f]
                if kind == "attT":
                    act.wait_ge(m_filled, M_FILLS * c + (f + 1))
                    nc.scalar.copy(attT[:, :, t * P:(t + 1) * P],
                                   bank_m(c, f)[:, 0:2 * P].rearrange("p (a n) -> p a n", a=2)).then_inc(attT_ready, 1)
                elif kind == "xn2T":
                    act.wait_ge(m_filled, M_FILLS * c + (f + 1))
                    nc.scalar.copy(xn2T_hi[:, t, :], bank_m(c, f)).then_inc(xn2T_high, 1)
                elif kind == "router":
                    act.wait_ge(rneg_ready, c + 1)
                    logits = bank_m(c, f)[:, 0:16 * QT].rearrange("p (t e) -> p t e", t=QT)
                    for i in range(QT):
                        nc.scalar.activation(e8[:, i, :], logits[:, i, 0:E], ACT.Exp, bias=rneg[:, i:i + 1])
                    nc.scalar.activation(ez[:, :], logits[:, :, E], ACT.Exp, scale=-1.0).then_inc(router_exp, 1)

            def step(s, par, next_a, first=False, last=False):
                f = m = 0
                for k in range(KT):
                    for h in range(HG):
                        i = HG * k + h
                        act.wait_ge(b_filled, EXPS * s + (i + 1))
                        if h == 0 and not (first and k < 2):
                            act.wait_ge(pv_done, KT * s + (k - 1))
                        nc.scalar.activation(probs[0:KW[k], (k + par) % 2, h, :], ps_b[0:KW[k], b_bank(i, par), :],
                                             ACT.Exp, scale=SCALE).then_inc(exp_done, 1)
                    if k == 0 and not first:
                        copy_out(s - 1)
                    if next_a:
                        for kind, g, _ in A_FILLS[f:f + A_SHARE[k]]:
                            if kind == "shift":
                                copy_shift(s + 1, g)
                        f += A_SHARE[k]
                    if last:
                        for m in LAST_SHARE[k]:
                            copy_m(0, m)

            step(0, 0, True, first=True)
            with act.Fori(0, STEPS // 2 - 1) as j:
                step(j * 2 + 1, 1, True)
                step(j * 2 + 2, 0, True)
            step(STEPS - 1, 1, False, last=True)
            copy_out(STEPS - 1)
            for f in range(M_AT["xn2T", 0], M_FILLS):
                if f not in LAST_FILLS:
                    copy_m(0, f)

            def hidden_high_of(c, u):
                act.wait_ge(h_ready, UNITS * c + (u + 1))
                if not (isinstance(c, int) and c == 0 and u < 4):
                    act.wait_ge(d_filled, QT * PAIRS * c + QT * (u // 2 - 1))
                nc.scalar.copy(hid_hi[:, u % 4, :], hid[u % 2][:, :]).then_inc(hidden_high, 1)

            def experts(c, next_m=True):
                for u in range(UNITS):
                    act.wait_ge(gu_filled, UNITS * c + (u + 1))
                    if not (isinstance(c, int) and c == 0 and u < 2):
                        act.wait_ge(h_ready, UNITS * c + (u - 1))
                    nc.scalar.activation(silu[:, u % 2, :], ps_a[:, 2 * (u % 2), :], ACT.Silu).then_inc(silu_done, 1)
                    if next_m and u == UNITS - 1:
                        copy_m(c + 1, M_AT["xn2T", 0])
                        copy_m(c + 1, M_AT["xn2T", 1])
                    hidden_high_of(c, u)
                    for f in M_AT_PLACE[u // 2][0:2] if u % 2 == 0 else M_AT_PLACE[u // 2][2:4]:
                        if next_m and f is not None:
                            copy_m(c + 1, f)
                if next_m:
                    copy_m(c + 1, M_AT["router", 0])

            experts(0)
            with act.Fori(1, NC - 1) as c:
                experts(c)
            experts(NC - 1, False)

        @block.vector
        def _(dve):
            done = [0, 0]

            def link(ins):
                done[0] += 1
                ins.then_inc(dve_chain, 1)
                hold(dve, dve_chain, done[1] + done[0], passed["dve"])

            def ln1_of(c):
                dve.wait_ge(x_loaded[c], 16)
                for t in range(QT):
                    nc.vector.bn_stats(stats[:, t, :], x_in[:, QT * c + t, :]).then_inc(dve_chain, 1)
                    done[0] += 1
                dve.wait_ge(dve_chain, done[0])
                for t in range(QT):
                    last = nc.vector.bn_aggr(mv1[:, QT * c + t, :], stats[:, t, :])
                last.then_inc(ln1_stats, 1)
                dve.wait_ge(ln1_rstd, c + 1)
                for t in range(QT * c, QT * (c + 1)):
                    last = nc.vector.tensor_scalar(x_in[:, t, :], x_in[:, t, :], mv1[:, t, 0:1], rstd1[:, t:t + 1],
                                                   ALU.subtract, ALU.mult)
                last.then_inc(ln1_done, 1)
                dve.wait_ge(ln1_done, c + 1)

            def split(what, ready):
                full, hi, mid, lo = parts_of(what)
                dve.wait_ge(*consumer(what))
                link(nc.vector.tensor_copy(hi, full))
                link(nc.vector.tensor_tensor(full, full, hi, ALU.subtract))
                link(nc.vector.tensor_copy(mid, full))
                nc.vector.tensor_tensor(lo, full, mid, ALU.subtract).then_inc(ready, 1)

            ln1_of(0)
            split(("k", KC - 1), k_split[0])
            split(("q", 1), q_split)
            for c in range(1, NC):
                ln1_of(c)

            def maximum(s, f):
                kind, u, j = A_FILLS[f]
                if kind == "shift":
                    return
                dve.wait_ge(a_filled, FILLS * s + (f + 1))
                n = KC * u + j
                nc.vector.reduce_max(piece_max[:, u, j:j + 1], ps_a[:, f % 4, 0:KPW[j]],
                                     axis=AX.X).then_inc(a_reduced, 1)
                if (n + 1) % (QT * KC) == 0:
                    h = u // QT
                    dve.wait_ge(a_reduced, HG * QT * KC * s + (n + 1))
                    nc.vector.tensor_reduce(neg_max[:, QT * h:QT * (h + 1)], piece_max[:, QT * h:QT * (h + 1), :],
                                            op=ALU.max, axis=AX.X, negate=True).then_inc(head_max, 1)

            dve.wait_ge(wv_loaded, 32)
            dve.wait_ge(v_ones, 1)
            for kind, what in FIRST_A:
                if kind == "a":
                    maximum(0, what)
                elif kind == "p" and what[0] == "v":
                    k, w = what[1], KW[what[1]]
                    dve.wait_ge(p_filled, PRO_AT[what] + 1)
                    nc.vector.tensor_tensor(v_all[0:w, :, k, :, 0:D],
                                            bank_p[PRO_AT[what] % 4][0:w, 0:C].rearrange("p (g h d) -> p g h d", g=G, h=HG),
                                            bv_s[0:w, :].rearrange("p (g h d) -> p g h d", g=G, h=HG),
                                            ALU.add).then_inc(v_copied, 1)
            with dve.Fori(1, STEPS) as s:
                for f in range(FILLS):
                    maximum(s, f)

            dve.wait_ge(wo_loaded, 16 * 5)
            link(nc.vector.tensor_copy(rt_hi[:, :, :], rt_w[:, :, :]))
            nc.vector.tensor_tensor(rt_lo[:, :, :], rt_w[:, :, :], rt_hi[:, :, :].bitcast(F32),
                                    ALU.subtract).then_inc(rt_split, 1)
            dve.wait_ge(ffw_loaded, 16 * 7)
            dve.wait_ge(pv_done, KT * (STEPS - 1))
            for w in W_SPLITS:
                nc.vector.tensor_copy(w_hi[w][:, :, :], w_raw[w][:, :, :]).then_inc(w_high, 1)

            def normalize(c, t):
                f = M_AT["att", t]
                dve.wait_ge(m_filled, M_FILLS * c + (f + 1))
                sums = bank_m(c, f).rearrange("p (h w) -> p h w", w=VW)
                link(nc.vector.reciprocal(rden[:, t, :], sums[:, :, D]))
                nc.vector.tensor_tensor(att[:, t, :].rearrange("p (h d) -> p h d", d=D), sums[:, :, 0:D],
                                        rden[:, t, :].unsqueeze(2).to_broadcast([P, H, D]), ALU.mult).then_inc(att_ready, 1)

            def residual(c, t):
                f = M_AT["proj", t]
                dve.wait_ge(m_filled, M_FILLS * c + (f + 1))
                dve.wait_ge(xb_ready, QT * c + (t + 1))
                nc.vector.scalar_tensor_tensor(x1[:, t, :], bank_m(c, f)[:, 0:C], tg[:, 0:1], xb[:, t, :],
                                               ALU.mult, ALU.add).then_inc(x1_ready, 1)
                dve.wait_ge(x1_ready, QT * c + (t + 1))
                link(nc.vector.bn_stats(stats[:, t, :], x1[:, t, :]))
                nc.vector.bn_aggr(mv2[:, t, :], stats[:, t, :]).then_inc(ln2_stats, 1)

            def norm2(c):
                dve.wait_ge(ln2_rstd, c + 1)
                for t in range(QT):
                    nc.vector.tensor_scalar(xn2[:, t, :], x1[:, t, :], mv2[:, t, 0:1], rstd2[:, t:t + 1],
                                            ALU.subtract, ALU.mult).then_inc(xn2_ready, 1)

            def xn2T_low_of(c, a):
                dve.wait_ge(xn2T_high, 2 * c + (a + 1))
                nc.vector.tensor_tensor(xn2T_lo[:, a, :], bank_m(c, M_AT["xn2T", a]), xn2T_hi[:, a, :].bitcast(F32),
                                        ALU.subtract).then_inc(xn2T_ready, 1)

            def logits_max(c):
                f = M_AT["router", 0]
                dve.wait_ge(m_filled, M_FILLS * c + (f + 1))
                logits = bank_m(c, f)[:, 0:16 * QT].rearrange("p (t e) -> p t e", t=QT)
                nc.vector.tensor_reduce(rneg[:, :], logits[:, :, 0:E], op=ALU.max, axis=AX.X,
                                        negate=True).then_inc(rneg_ready, 1)

            def route(c):
                hold(dve, router_exp, c + 1, passed["dve"])
                for t in range(QT):
                    ins = nc.vector.max(v8[:, t, :], e8[:, t, :])
                link(ins)
                for t in range(QT):
                    ins = nc.vector.max_index(i8[:, t, :], v8[:, t, :], e8[:, t, :])
                link(ins)
                link(nc.vector.tensor_copy(i2[:, :, :], i8[:, :, 0:2]))
                link(nc.vector.tensor_tensor(s2[:, :], v8[:, :, 0], v8[:, :, 1], ALU.add))
                link(nc.vector.reciprocal(r2[:, :], s2[:, :]))
                link(nc.vector.tensor_scalar(r2[:, :], r2[:, :], tg[:, 1:2], None, ALU.mult))
                link(nc.vector.tensor_tensor(w2[:, :, :], v8[:, :, 0:2], r2[:, :].unsqueeze(2).to_broadcast([P, QT, 2]),
                                             ALU.mult))
                for t in range(QT):
                    for n, half in enumerate((cwa, cwb)):
                        last = nc.vector.tensor_scalar(half[:, t, :], iota[:, :], i2[:, t, n:n + 1], w2[:, t, n:n + 1],
                                                       ALU.is_equal, ALU.mult)
                link(last)
                link(nc.vector.tensor_tensor(cw[:, :, 0:E], cwa[:, :, :], cwb[:, :, :], ALU.add))
                link(nc.vector.tensor_scalar(ez[:, :], ez[:, :], 1.0, None, ALU.add))
                link(nc.vector.reciprocal(s2[:, :], ez[:, :]))
                link(nc.vector.tensor_scalar(cw[:, :, E], s2[:, :], tg[:, 1:2], None, ALU.mult))

            def hidden_of(c, u):
                dve.wait_ge(silu_done, UNITS * c + (u + 1))
                if not (isinstance(c, int) and c == 0 and u < 2):
                    dve.wait_ge(hidden_low, UNITS * c + (u - 1))
                nc.vector.tensor_tensor(hid[u % 2][:, :], silu[:, u % 2, :], ps_a[:, 2 * (u % 2) + 1, :],
                                        ALU.mult).then_inc(h_ready, 1)

            def combine(c, pair, t):
                d = QT * pair + t
                dve.wait_ge(d_filled, QT * PAIRS * c + (d + 1))
                if pair == 0:
                    wait(dve, stored[t], 16 * c)
                else:
                    dve.wait_ge(combined, QT * PAIRS * c + (d + 1 - QT))
                bank = bank_d[d % 2]
                so_far = x1 if pair == 0 else res
                if pair < E // 2:
                    link(nc.vector.scalar_tensor_tensor(res[:, t, :], bank[:, 0:C], cw[:, t, 2 * pair:2 * pair + 1],
                                                        so_far[:, t, :], ALU.mult, ALU.add))
                    ins = nc.vector.scalar_tensor_tensor(res[:, t, :], bank[:, C:2 * C],
                                                         cw[:, t, 2 * pair + 1:2 * pair + 2],
                                                         res[:, t, :], ALU.mult, ALU.add)
                else:
                    ins = nc.vector.scalar_tensor_tensor(res[:, t, :], bank[:, 0:C], cw[:, t, E:E + 1],
                                                         res[:, t, :], ALU.mult, ALU.add)
                ins.then_inc(combined, 1)

            def work_m(c, f):
                kind, t = M_ORDER[f]
                if kind == "att":
                    normalize(c, t)
                elif kind == "proj":
                    residual(c, t)

            def experts(c, next_m=True, before=True):
                for pair in range(PAIRS):
                    def place(t):
                        if pair or before:
                            combine(c if pair else c - 1, (pair - 1) % PAIRS, t)
                        if next_m and M_AT_PLACE[pair][t] is not None:
                            work_m(c + 1, M_AT_PLACE[pair][t])

                    if pair == PAIRS - 1 and next_m:
                        norm2(c + 1)
                    hidden_of(c, 2 * pair)
                    place(0)
                    place(1)
                    hidden_of(c, 2 * pair + 1)
                    if pair == PAIRS - 1 and next_m:
                        xn2T_low_of(c + 1, 0)
                        xn2T_low_of(c + 1, 1)
                    place(2)
                    place(3)
                    if pair == 0:
                        route(c)
                if next_m:
                    logits_max(c + 1)

            dve.wait_ge(tanh_done, 1)
            for f in range(M_AT["xn2T", 0]):
                work_m(0, f)
            norm2(0)
            xn2T_low_of(0, 0)
            xn2T_low_of(0, 1)
            logits_max(0)
            before_chunk = done[0]
            experts(0, before=False)
            start, per_chunk = done[0], done[0] - before_chunk
            with dve.Fori(1, NC - 1) as c:
                done[0], done[1] = 0, (c - 1) * per_chunk + start
                experts(c)
            done[0], done[1] = start + (NC - 2) * per_chunk, 0
            experts(NC - 1, False)
            for t in range(QT):
                combine(NC - 1, PAIRS - 1, t)

        @block.tensor
        def _(pe):
            mm = nc.tensor.matmul

            def transpose(out_, in_):
                return mm(out_, in_, ident[:, :], start=True, stop=True, is_transpose=True)

            def project(what):
                kind, n = what
                at_ = PRO_AT[what]
                bank = bank_p[at_ % 4]
                if at_ >= 4:
                    pe.wait_ge(*consumer(PRO[at_ - 4]))
                if kind == "k":
                    a, j = n // KC, n % KC
                    if a == 0:
                        pe.wait_ge(ctx_loaded[j], 16)
                    for i in range(2):
                        last = mm(bank[:, 0:KPW[j]], wk_s[:, i, a * P:(a + 1) * P],
                                  ctx_in[:, i, KP0[j]:KP0[j] + KPW[j]], start=(i == 0), stop=(i == 1))
                elif kind == "x":
                    c, a = n // 2, n % 2
                    pe.wait_ge(ln1_done, c + 1)
                    for t in range(QT):
                        last = transpose(bank[:, t * P:(t + 1) * P], x_in[:, QT * c + t, a * P:(a + 1) * P])
                elif kind == "q":
                    c, a = n // 2, n % 2
                    pe.wait_ge(xnT_copied, 2 * c + 2)
                    for i in range(2):
                        last = mm(bank, wq_s[:, i, a * P:(a + 1) * P], xnT[:, i, :], start=(i == 0), stop=(i == 1))
                else:
                    for i in range(2):
                        last = mm(bank[0:KW[n], 0:C], ctx_in[:, i, n * P:n * P + KW[n]], wv_s[:, i, :],
                                  start=(i == 0), stop=(i == 1))
                last.then_inc(p_filled, 1)

            pe.wait_ge(wk_loaded, 32)
            for what in PRO_FIRST:
                if what == ("x", 0):
                    pe.wait_ge(consts_made, 1)
                if what == ("q", 0):
                    pe.wait_ge(wq_loaded, 32)
                project(what)

            def fill_a(s, f, first=False):
                kind, u, j = A_FILLS[f]
                if not (first and f < 4):
                    back, prev = (0, f - 4) if f >= 4 else (1, f - 4 + FILLS)
                    pkind, pu, pj = A_FILLS[prev]
                    if pkind == "score":
                        pe.wait_ge(a_reduced, HG * QT * KC * s + (KC * pu + pj + 1 - back * HG * QT * KC))
                    else:
                        pe.wait_ge(shift_copied, HG * s + (pu + 1 - back * HG))
                if kind == "score":
                    h, t = u // QT, u % QT
                    mm(ps_a[:, f % 4, 0:KPW[j]], queries(s, h, t * P, P, 0, SPLIT), keys(s, h, KP0[j], KPW[j], SPLIT),
                       start=True, stop=True).then_inc(a_filled, 1)
                else:
                    pe.wait_ge(shift_low, HG * s + (u + 1))
                    for t in range(QT):
                        last = mm(ps_a[SPLIT:ROWS, f % 4, t * P:(t + 1) * P], shift[:, QT * u + t, :], ident_b[:, :],
                                  start=True, stop=True)
                    last.then_inc(a_filled, 1)

            def begin_a(s, par):
                pe.wait_ge(q_staged[par], 6 * 16 * (s // 2) + 6 * 16)
                pe.wait_ge(k_staged, 6 * 16 * (s // NC) + 6 * 16)

            def probs_times_v(s, par, k, first=False):
                pe.wait_ge(exp_done, EXPS * s + HG * (k + 1))
                if k == 0:
                    pe.wait_ge(v_staged[par], 16 * (s // 2) + 16)
                    if not first:
                        pe.wait_ge(out_copied, s)
                for h in range(HG):
                    last = mm(ps_o[VW * h:VW * (h + 1), :], v_use[par][0:KW[k], k, h, :],
                              probs[0:KW[k], (k + par) % 2, h, :], start=(k == 0), stop=(k == KT - 1))
                last.then_inc(pv_done, 1)

            def step(s, par, next_a, first=False, last=False):
                if next_a:
                    begin_a(s + 1, 1 - par)
                f = 0
                for k in range(KT):
                    share = A_SHARE[k] if next_a else 0
                    for h in range(HG):
                        i = HG * k + h
                        if not (first and i < 3):
                            pe.wait_ge(exp_done, EXPS * s + b_bank_used(i, par))
                        if k == 0:
                            pe.wait_ge(shift_copied, HG * s + (h + 1))
                        mm(ps_b[0:KW[k], b_bank(i, par), :], keys(s, h, k * P, KW[k]), queries(s, h, 0, QC),
                           start=True, stop=True).then_inc(b_filled, 1)
                        n = share * (h + 1) // HG
                        while share > 1 and f < sum(A_SHARE[:k]) + n:
                            fill_a(s + 1, f)
                            f += 1
                    if k:
                        probs_times_v(s, par, k - 1, first)
                    elif not first:
                        probs_times_v(s - 1, 1 - par, KT - 1)
                    if share == 1:
                        fill_a(s + 1, f)
                        f += 1
                    if last:
                        for m in LAST_SHARE[k]:
                            fill_m(0, m)

            def fill_m(c, f):
                kind, t = M_ORDER[f]
                if isinstance(c, int) and c < 2 and f < 2:
                    if c == 0:
                        pe.wait_ge(a_reduced, HG * QT * KC * STEPS)
                        pe.wait_ge(shift_copied, HG * STEPS)
                        pe.wait_ge(outT_loaded, 16)
                        pe.wait_ge(wo_loaded, 16 * 5)
                        pe.wait_ge(rt_split, 1)
                    else:
                        pe.wait_ge(out_copied, STEPS)
                else:
                    back, prev = (0, f - 2) if f >= 2 else (1, max(g for g in range(M_FILLS) if g % 2 == f % 2))
                    pkind, pt = M_ORDER[prev]
                    gone, each = {"att": (att_ready, QT), "attT": (attT_ready, QT), "proj": (x1_ready, QT),
                                  "xn2T": (xn2T_ready, 2), "router": (router_exp, 1)}[pkind]
                    pe.wait_ge(gone, each * c + (pt + 1 - back * each))
                bank = bank_m(c, f)
                if kind == "att":
                    pe.wait_ge(outT_loaded, 16 * c + 16)
                    for g in range(G):
                        last = transpose(bank[:, g * P:(g + 1) * P], outT[:, g, t * P:(t + 1) * P])
                elif kind == "attT":
                    pe.wait_ge(att_ready, QT * c + (t + 1))
                    for a in range(2):
                        last = transpose(bank[:, a * P:(a + 1) * P], att[:, t, a * P:(a + 1) * P])
                elif kind == "proj":
                    pe.wait_ge(attT_ready, QT * c + (t + 1))
                    for a in range(2):
                        last = mm(bank[:, 0:C], attT[:, a, t * P:(t + 1) * P], wo_s[:, a, :],
                                  start=(a == 0), stop=(a == 1))
                elif kind == "xn2T":
                    pe.wait_ge(xn2_ready, QT * c + QT)
                    for i in range(QT):
                        last = transpose(bank[:, i * P:(i + 1) * P], xn2[:, i, t * P:(t + 1) * P])
                else:
                    pe.wait_ge(xn2T_ready, 2 * c + 2)
                    for i in range(QT):
                        for a in range(2):
                            for n, (xx, ww) in enumerate(((xn2T_hi, rt_hi), (xn2T_hi, rt_lo), (xn2T_lo, rt_hi))):
                                last = mm(bank[:, 16 * i:16 * i + E + 2], xx[:, a, i * P:(i + 1) * P], ww[:, a, :],
                                          start=(a == n == 0), stop=(a == 1 and n == 2))
                last.then_inc(m_filled, 1)

            pe.wait_ge(wv_loaded, 32)
            begin_a(0, 0)
            for kind, what in FIRST_A:
                if kind == "a":
                    fill_a(0, what, first=True)
                elif kind == "p":
                    project(what)
            pe.wait_ge(key_ones, 1)
            for n in range(len(PRO) - 4, len(PRO)):
                pe.wait_ge(*consumer(PRO[n]))
            step(0, 0, True, first=True)
            with pe.Fori(0, STEPS // 2 - 1) as j:
                step(j * 2 + 1, 1, True)
                step(j * 2 + 2, 0, True)
            step(STEPS - 1, 1, False, last=True)
            probs_times_v(STEPS - 1, 1, KT - 1)
            for f in range(M_FILLS):
                if f not in LAST_FILLS:
                    fill_m(0, f)

            def gate_up(c, u, n):
                if n == 0:
                    if not (isinstance(c, int) and c == 0 and u < 2):
                        pe.wait_ge(h_ready, UNITS * c + (u - 1))
                    if u == 0:
                        pe.wait_ge(xn2T_ready, 2 * c + 2)
                    if isinstance(c, int) and c == 0:
                        if u == 1:
                            pe.wait_ge(router_exp, 1)
                        pe.wait_ge(w_low, 1 if u < 4 else 3 if u < E else 6)
                name = ("gu0" if u < E // 2 else "gu1") if u < E else ("sg", "su")[n]
                at_ = 2 * I * (u % (E // 2)) + I * n if u < E else P * (u - E)
                for a in range(2):
                    for m, (ww, xx) in enumerate(((w_hi, xn2T_hi), (w_hi, xn2T_lo), (w_lo, xn2T_hi))):
                        last = mm(ps_a[:, 2 * (u % 2) + n, :], ww[name][:, a, at_:at_ + P], xx[:, a, :],
                                  start=(a == m == 0), stop=(a == 1 and m == 2))
                if n:
                    last.then_inc(gu_filled, 1)

            def down(c, pair, t):
                if t == 0:
                    pe.wait_ge(hidden_low, UNITS * c + 2 * (pair + 1))
                    if isinstance(c, int) and c == 0:
                        pe.wait_ge(w_low, 2 if pair < 2 else 4 if pair < 4 else 7)
                d = QT * pair + t
                if not (isinstance(c, int) and c == 0 and d < 2):
                    pe.wait_ge(combined, QT * PAIRS * c + (d - 1))
                for n in range(2):
                    u = 2 * pair + n
                    name = ("dw0" if u < E // 2 else "dw1") if u < E else "sd"
                    row = u % (E // 2) if u < E else u - E
                    cols = slice(n * C, (n + 1) * C) if u < E else slice(0, C)
                    for m, (hh, ww) in enumerate(((hid_hi, w_hi), (hid_hi, w_lo), (hid_lo, w_hi))):
                        last = mm(bank_d[d % 2][:, cols], hh[:, u % 4, t * P:(t + 1) * P], ww[name][:, row, :],
                                  start=(m == 0 and (u < E or n == 0)), stop=(m == 2 and (u < E or n == 1)))
                last.then_inc(d_filled, 1)

            def experts(c, next_m=True, before=True):
                for pair in range(PAIRS):
                    def place(t):
                        if pair or before:
                            down(c if pair else c - 1, (pair - 1) % PAIRS, t)
                        if next_m and M_AT_PLACE[pair][t] is not None:
                            fill_m(c + 1, M_AT_PLACE[pair][t])

                    gate_up(c, 2 * pair, 0)
                    gate_up(c, 2 * pair, 1)
                    place(0)
                    gate_up(c, 2 * pair + 1, 0)
                    place(1)
                    gate_up(c, 2 * pair + 1, 1)
                    if pair == PAIRS - 1 and next_m:
                        fill_m(c + 1, M_AT["xn2T", 0])
                        fill_m(c + 1, M_AT["xn2T", 1])
                    place(2)
                    place(3)
                if next_m:
                    fill_m(c + 1, M_AT["router", 0])

            experts(0, before=False)
            with pe.Fori(1, NC - 1) as c:
                experts(c)
            experts(NC - 1, False)
            for t in range(QT):
                down(NC - 1, PAIRS - 1, t)


def kernel(x, ctx_1024, g_xattn, g_ffn, L0_xattn_Wq, L0_xattn_bq, L0_xattn_Wk, L0_xattn_bk, L0_xattn_Wv,
           L0_xattn_bv, L0_xattn_Wo, L0_xattn_bo, L0_ffn_router_weight, L0_ffn_gate_up_proj, L0_ffn_down_proj,
           L0_ffn_shared_gate_w, L0_ffn_shared_up_w, L0_ffn_shared_down_w, L0_ffn_shared_expert_gate_w):
    import numpy as np
    import concourse.bacc as bacc
    from concourse.bass_utils import run_bass_kernel_spmd

    def cols(w):
        w = np.asarray(w)
        return np.ascontiguousarray(w.T.reshape(-1, P, w.shape[0]).transpose(1, 0, 2))

    order = np.arange(C).reshape(2, 2, HG, D).transpose(0, 1, 3, 2).reshape(-1)
    arrays = {
        "x": np.ascontiguousarray(np.asarray(x)[0]),
        "ctxT": np.ascontiguousarray(np.asarray(ctx_1024)[0].T.reshape(2, P, NK).transpose(1, 0, 2)),
        "wq": cols(np.asarray(L0_xattn_Wq)[order]), "wk": cols(np.asarray(L0_xattn_Wk)[order]),
        "wv": cols(L0_xattn_Wv), "wo": cols(L0_xattn_Wo),
        "bq": np.ascontiguousarray(np.asarray(L0_xattn_bq)[order].reshape(2, P).T),
        "bk": np.ascontiguousarray(np.asarray(L0_xattn_bk)[order].reshape(2, P).T),
        "bv": np.asarray(L0_xattn_bv), "bo": np.asarray(L0_xattn_bo),
        "g_x": np.asarray(g_xattn), "g_f": np.asarray(g_ffn),
        "router": cols(np.concatenate([np.asarray(L0_ffn_router_weight), np.asarray(L0_ffn_shared_expert_gate_w)])),
        "gu": cols(np.asarray(L0_ffn_gate_up_proj).reshape(E * 2 * I, C)),
        "dw": np.ascontiguousarray(np.asarray(L0_ffn_down_proj).transpose(2, 0, 1)),
        "sg": cols(L0_ffn_shared_gate_w), "su": cols(L0_ffn_shared_up_w), "sd": cols(L0_ffn_shared_down_w),
    }
    nc = bacc.Bacc("TRN2", target_bir_lowering=False, num_devices=1)
    aps = [nc.dram_tensor(f"in_{n}", a.shape, mybir.dt.from_np(a.dtype), kind="ExternalInput").ap()
           for n, a in arrays.items()]
    result = nc.dram_tensor("result", (NT, C), F32, kind="ExternalOutput").ap()
    flamingo_block(nc, *aps, result)
    got = run_bass_kernel_spmd(nc, [{f"in_{n}": a for n, a in arrays.items()}], core_ids=[0])
    return got.results[0]["result"].reshape(1, NT, C)
```

```python
from contextlib import ExitStack

import concourse.bass as bass
from concourse import mybir

F32 = mybir.dt.float32
F32R = mybir.dt.float32r
BF16 = mybir.dt.bfloat16
U32 = mybir.dt.uint32
ALU = mybir.AluOpType
ACT = mybir.ActivationFunctionType
AX = mybir.AxisListType

P = 128
C = 256
NT = 2048
NK = 1601
H, D = 16, 16
HG = 4
G = H // HG
QC = 512
NC = NT // QC
QT = QC // P
STEPS = G * NC
KT = -(-NK // P)
KW = [min(P, NK - P * k) for k in range(KT)]
KC = 4
KP0 = [401 * j - max(0, j - 1) for j in range(KC)]
KPW = [401] + [400] * (KC - 1)
SPLIT = 6 * D
ROWS = SPLIT + 2
VW = 32
SCALE = D ** -0.5
EPS = 1e-5
E, I, SI = 8, 128, 512
UNITS = E + SI // P
PAIRS = UNITS // 2
ROUTE_W = 2 * (E + 2)

FILLS = QT * HG * KC + HG
EXPS = KT * HG
Q_PARTS = [0, 0, 0, 1, 1, 2]
K_PARTS = [0, 1, 2, 0, 1, 0]


def pass_a_fills():
    out, due = [], []
    for i in range(HG * QT * KC):
        out.append(("score", i // KC, i % KC))
        if (i + 1) % (QT * KC) == 0:
            due.append((i + 4, i // (QT * KC)))
        if due and i == due[0][0]:
            out.append(("shift", due.pop(0)[1], 0))
    return out + [("shift", h, 0) for _, h in due]


A_FILLS = pass_a_fills()
A_SHARE = [6, 6, 5, 6, 6, 5, 6, 6, 5, 6, 5, 5, 1]
assert sum(A_SHARE) == FILLS == len(A_FILLS)
SHIFT_AT = [A_FILLS.index(("shift", h, 0)) for h in range(HG)]



V_EARLY = 8
ONES_EARLY = 6
LATER = ([("v", k) for k in range(V_EARLY, KT)]
         + [(kind, 2 * c + a) for c in range(1, NC) for kind in "xq" for a in range(2)]
         + [("k", KC + j) for j in range(KC)])
LN_AT = {10: ("norm", 2), 20: ("stats", 3), 30: ("norm", 3)}
COST = {"v": 2, "x": 2, "q": 4, "k": 3}


def projection_order():
    out = [("stats", 0), ("norm", 0)]
    out += [("p", what) for what in (("k", 0), ("x", 0), ("x", 1), ("k", 1), ("q", 0), ("q", 1), ("k", 2), ("k", 3))]
    out += [("split", ("k", KC - 1)), ("mid", ("k", KC - 1)), ("split", ("q", 1)), ("stats", 1), ("stats", 2), ("norm", 1)]
    out += [("p", ("v", k)) for k in range(V_EARLY)]
    later, due, spent = list(LATER), [], 0
    for f in range(FILLS):
        if f in LN_AT:
            out.append(LN_AT[f])
        kind, u, j = A_FILLS[f]
        if later and (kind == "shift" or len(later) > 1 and spent * FILLS <= f * sum(COST[k] for k, _ in LATER)):
            what = later.pop(0)
            spent += COST[what[0]]
            out.append(("p", what))
            if what[0] == "q" and what[1] % 2:
                out.append(("split", what))
                due.append((f + 8, what))
        out.append(("a", f))
        if kind == "score" and (u + 1) % QT == 0 and j == KC - 1:
            out.append(("max", u // QT))
        if due and f >= due[0][0]:
            out.append(("mid", due.pop(0)[1]))
    assert not later and not due
    return out


ORDER = projection_order()
P_FILLS = [what for kind, what in ORDER if kind == "p"]
PRO_AT = {what: n for n, what in enumerate(P_FILLS)}
FIRST_K, LAST_K = ("k", KC - 1), ("k", 2 * KC - 1)

M_ORDER = [("att", 0), ("att", 1), ("attT", 0), ("att", 2), ("attT", 1), ("proj", 0), ("att", 3), ("attT", 2),
           ("proj", 1), ("attT", 3), ("proj", 2), ("proj", 3), ("xn2T", 0), ("xn2T", 1), ("router", 0)]
M_FILLS = len(M_ORDER)
M_AT = {what: f for f, what in enumerate(M_ORDER)}
M_AT_PLACE = [[0, 1, None, 2], [3, None, 4, 5], [6, 7, None, 8], [9, None, 10, None], [11, None, None, None],
              [None] * QT]
LAST_PLACES = [(None, 0), (1, 2), (3, 4), (5, 6), (7, 8), (9, 10), (11, None), (None, None), (None, None),
               (12, 13), (None, None), (14, None), (None, None)]
W_SPLITS = ["gu0", "dw0", "gu1", "dw1", "sg", "su", "sd"]


def wait(eng, sem, value):
    if not (isinstance(value, int) and value <= 0):
        eng.wait_ge(sem, value)


def hold(eng, sem, value, passed):
    eng.wait_ge(sem, value)
    eng.sem_inc(passed, 1)


def flamingo_block(nc, x, ctxT, wq, wk, wv, wo, bq, bk, bv, bo, g_x, g_f, router, gu, dw, sg, su, sd, out):
    with ExitStack() as ctx:
        def sb(name, shape, dt=F32):
            return ctx.enter_context(nc.sbuf_tensor(name, shape, dt))

        def sem(name):
            return ctx.enter_context(nc.semaphore(name))

        SPLITW = 3 * 2 * NT + 3 * 2 * NK
        VG = KT * HG * VW
        KSW = HG * NK
        sizes = {"parts": 2 * SPLITW, "v_all": 4 * G * VG, "v0": 4 * VG, "v1": 4 * VG, "k_stack": 2 * 2 * KSW,
                 "q_stack": 2 * NC * HG * QC, "probs": 4 * 2 * HG * QC, "big": 4 * STEPS * QC,
                 "temp": 4 * (G + 4) * QC, "xnT": 4 * 2 * QC}
        sizes = {n: -(-b // 32) * 32 + (5 * 32 if n == "parts" else 0) for n, b in sizes.items()}
        base = -(-nc.sbuf_base // 32) * 32
        slab = sb("slab", [P, sum(sizes.values()) // 4])
        region = {}
        for n, b in sizes.items():
            region[n], base = [base, base + b], base + b

        def at(where, name, shape, dt=F32):
            width = 4 if dt in (F32, F32R) else 2
            for n in shape[1:]:
                width *= n
            lo, hi = region[where]
            at_ = used.get(where, lo)
            used[where] = -(-(at_ + width) // 32) * 32
            assert at_ + width <= hi, (name, at_ + width - hi)
            return nc.alloc_sbuf_tensor_at(name, shape, dt, offset=at_)

        used = {}
        q_part = [at("parts", f"q_part{i}", [P, 2, NT], BF16) for i in range(3)]
        k_part = [at("parts", f"k_part{i}", [P, 2, NK], BF16) for i in range(3)]
        v_mem = at("v_all", "v_all", [P, G * VG])
        v_all = v_mem[:, :].rearrange("p (g k h w) -> p g k h w", g=G, k=KT, h=HG)
        v_grp = [at(f"v{i}", f"v_group{i}", [P, VG]) for i in range(2)]
        v_use = [v[:, :].rearrange("p (k h w) -> p k h w", k=KT, h=HG) for v in v_grp]
        k_stack = at("k_stack", "k_stack", [P, 2 * KSW], BF16)
        q_stack = at("q_stack", "q_stack", [P, NC * HG * QC], BF16)
        probs = at("probs", "probs", [P, 2, HG, QC])
        big = at("big", "attention_out", [P, STEPS * QC])
        k_full = at("temp", "k_full", [P, 2, NK])
        xnT = at("xnT", "xnT", [P, 2, QC])
        used = {}
        x_in = at("big", "x_in", [P, 16, C])
        q_full = at("probs", "q_full", [P, NC, 2, QC])
        ctx_in = at("big", "ctx_in", [P, 2, NK])
        w_raw = {"gu0": at("parts", "gu0", [P, 2, E * I]), "gu1": at("parts", "gu1", [P, 2, E * I]),
                 "dw0": at("parts", "dw0", [P, E // 2, C]), "dw1": at("parts", "dw1", [P, E // 2, C]),
                 "sg": at("parts", "sg", [P, 2, SI]), "su": at("parts", "su", [P, 2, SI]),
                 "sd": at("parts", "sd", [P, SI // P, C])}
        used = {}
        w_lo = {n: at("parts", n + "_lo", list(w_raw[n].shape), F32R)
                for n in ("gu0", "gu1", "dw0", "dw1", "sg", "su", "sd")}
        where = {"gu0": "k_stack", "dw0": "k_stack", "gu1": "q_stack", "dw1": "q_stack", 
                 "sg": "v0", "su": "xnT", "sd": "parts"}
        w_hi = {n: at(where[n], n + "_hi", list(w_raw[n].shape), F32R) for n in where}
        xb, x1, res, xn2, att = (at("v_all", n, [P, QT, C]) for n in ("x_again", "x1", "res", "xn2", "att"))
        attT = at("v_all", "attT", [P, 2, QC])
        outT = at("temp", "outT", [P, G, QC])
        xn2T_hi, xn2T_lo = (at("temp", n, [P, 2, QC], F32R) for n in ("xn2T_hi", "xn2T_lo"))
        silu = at("v1", "silu", [P, 2, QC])
        hid = [at(f"v{i}", f"hidden{i}", [P, QC]) for i in range(2)]
        hid_hi, hid_lo = (at("probs", n, [P, 4, QC], F32R) for n in ("hidden_hi", "hidden_lo"))

        wq_s, wk_s, wv_s, wo_s = (sb(n, [P, 2, C]) for n in ("wq", "wk", "wv", "wo"))
        bq_s, bk_s = sb("bq", [P, 2]), sb("bk", [P, 2])
        bv_s, bo_s = sb("bv", [P, C]), sb("bo", [P, C])
        rt_w = sb("router", [P, 2, E + 2])
        rt_parts = sb("router_parts", [P, 2, 2, E + 2], F32R)
        logits = sb("logits", [P, QT, E + 2])
        gates = sb("gates", [P, 2])
        tg = sb("tanh_gates", [P, 2])
        ident = sb("ident", [P, P])
        ident_b = sb("ident_b", [P, P], BF16)
        mhalf = sb("minus_half", [P, QT])
        iota = sb("iota", [P, E])
        stats = sb("stats", [P, QT, 6])
        mv1 = sb("mean_var1", [P, 16, 2])
        rstd1 = sb("rstd1", [P, 16])
        piece_max = sb("piece_max", [P, HG * QT, KC])
        neg_max = sb("neg_max", [P, HG * QT])
        shift = sb("shift_parts", [P, HG * QT, 2], BF16)
        rden = sb("rden", [P, QT, H])
        mv2 = sb("mean_var2", [P, QT, 2])
        rstd2 = sb("rstd2", [P, QT])
        rneg = sb("router_neg_max", [P, QT])
        e8 = sb("router_exp", [P, QT, E])
        ez = sb("gate_exp", [P, QT])
        v8 = sb("top_values", [P, QT, 8])
        i8 = sb("top_index", [P, QT, 8], U32)
        i2 = sb("top2_index", [P, QT, 2])
        s2 = sb("top2_sum", [P, QT, 2])
        r2 = sb("top2_scale", [P, QT, 2])
        w2 = sb("top2_weight", [P, QT, 2])
        cw2 = sb("weights_of_two", [P, QT, 2, E])
        cw = sb("weights", [P, QT, E])

        ps_a = ctx.enter_context(nc.psum_tensor("ps_a", [P, 4, 512], F32))
        ps_b = ctx.enter_context(nc.psum_tensor("ps_b", [P, 3, 512], F32))
        ps_o = ctx.enter_context(nc.psum_tensor("ps_o", [P, 512], F32))
        bank_p = [ps_b[:, 0, :], ps_b[:, 1, :], ps_b[:, 2, :], ps_o[:, :]]

        def bank_m(c, f):
            return ps_a[:, 2 + f % 2, :] if isinstance(c, int) and c == 0 else (ps_b[:, 2, :], ps_o[:, :])[f % 2]

        bank_d = [ps_b[:, 0, :], ps_b[:, 1, :]]

        x_loaded = [sem(f"x_loaded{c}") for c in range(NC)]
        ctx_loaded = [sem(f"ctx_loaded{j}") for j in range(KC)]
        wk_loaded, wq_loaded = sem("wk_loaded"), sem("wq_loaded")
        wv_loaded, wo_loaded = sem("wv_loaded"), sem("wo_loaded")
        consts_made, pool_chain, dve_chain = sem("consts_made"), sem("pool_chain"), sem("dve_chain")
        ln1_stats, ln1_rstd, ln1_done = sem("ln1_stats"), sem("ln1_rstd"), sem("ln1_done")
        xnT_copied, v_ones = sem("xnT_copied"), sem("v_ones")
        key_ones, w_high, w_low, h_ready = sem("key_ones"), sem("w_high"), sem("w_low"), sem("h_ready")
        p_filled, k_copied = sem("p_filled"), sem("k_copied")
        k_off, q_off = [sem(f"k_high_off{a}") for a in range(2)], [sem(f"q_high_off{c}") for c in range(NC)]
        k_high, q_high, v_filled_out = sem("k_high"), sem("q_high"), sem("v_filled_out")
        k_mid, k_split = [sem(f"k_mid{a}") for a in range(2)], [sem(f"k_split{a}") for a in range(2)]
        q_mid, q_split = [sem(f"q_mid{c}") for c in range(NC)], [sem(f"q_split{c}") for c in range(NC)]
        q_copied = sem("q_copied")
        v_copied = sem("v_copied")
        k_staged, q_staged, v_staged = sem("k_staged"), [sem("q_staged0"), sem("q_staged1")], [sem("v_staged0"), sem("v_staged1")]
        a_filled, a_reduced, head_max = sem("a_filled"), sem("a_reduced"), sem("head_max")
        shift_high, shift_low, shift_copied = sem("shift_high"), sem("shift_low"), sem("shift_copied")
        b_filled, exp_done, pv_done, out_copied = sem("b_filled"), sem("exp_done"), sem("pv_done"), sem("out_copied")
        tanh_done, bo_scaled = sem("tanh_done"), sem("bo_scaled")
        ffw_loaded, outT_loaded, xb_loaded, xb_ready = sem("ffw_loaded"), sem("outT_loaded"), sem("xb_loaded"), sem("xb_ready")
        m_filled, att_ready, attT_ready, x1_ready = sem("m_filled"), sem("att_ready"), sem("attT_ready"), sem("x1_ready")
        ln2_stats, ln2_eps, ln2_rstd, xn2_ready = sem("ln2_stats"), sem("ln2_eps"), sem("ln2_rstd"), sem("xn2_ready")
        xn2T_high, rt_split = sem("xn2T_high"), sem("rt_split")
        logits_ready = sem("logits_ready")
        xn2T_ready, rneg_ready, router_exp = sem("xn2T_ready"), sem("rneg_ready"), sem("router_exp")
        gu_filled, silu_done = sem("gu_filled"), sem("silu_done")
        hidden_high, hidden_low = sem("hidden_high"), sem("hidden_low")
        passed = {"pool": sem("pool_passed"), "dve": sem("dve_passed")}
        d_filled, combined, stored = sem("d_filled"), sem("combined"), [sem(f"stored{t}") for t in range(QT)]

        def keys(s, h, k0, n, rows=ROWS):
            at = (s // NC) % 2 * KSW + (h * NK + k0)
            return k_stack[0:rows, at:at + n] if isinstance(at, int) else k_stack[0:rows, bass.ds(at, n)]

        def queries(s, h, q0, n, lo=0, hi=ROWS):
            at = (s % NC) * (HG * QC) + (h * QC + q0)
            return q_stack[lo:hi, at:at + n] if isinstance(at, int) else q_stack[lo:hi, bass.ds(at, n)]

        def out_at(s):
            return big[:, s * QC:(s + 1) * QC] if isinstance(s, int) else big[:, bass.ds(s * QC, QC)]

        def b_bank(i, par):
            return (i + (2 if par else int(i >= HG * (KT // 2)))) % 3

        def b_bank_used(i, par):
            here = [j for j in range(i) if b_bank(j, par) == b_bank(i, par)]
            before = [j for j in range(EXPS) if b_bank(j, 1 - par) == b_bank(i, par)]
            return here[-1] + 1 if here else before[-1] + 1 - EXPS

        def consumer(what):
            kind, n = what
            return {"k": k_copied, "x": xnT_copied, "q": q_copied, "v": v_filled_out}[kind], n + 1

        def parts_of(what):
            kind, n = what
            if kind == "q":
                c = n // 2
                return q_full[:, c, :, :], *(p[:, :, c * QC:(c + 1) * QC] for p in q_part)
            a = n // KC
            return k_full[:, a, :], *(p[:, a, :] for p in k_part)

        def split_sems(what):
            kind, n = what
            i, sems = (n // 2, (q_off, q_mid, q_split)) if kind == "q" else (n // KC, (k_off, k_mid, k_split))
            return [each[i] for each in sems]

        block = ctx.enter_context(nc.Block())

        @block.sync
        def _(sp):
            x_chunks = x.rearrange("(c t p) n -> c p t n", c=NC, p=P)
            def load_ctx(j):
                sp.dma_start(ctx_in[:, :, KP0[j]:KP0[j] + KPW[j]],
                             ctxT[:, :, KP0[j]:KP0[j] + KPW[j]]).then_inc(ctx_loaded[j], 16)

            sp.dma_start(x_in[:, 0:QT, :], x_chunks[0]).then_inc(x_loaded[0], 16)
            sp.dma_start(wk_s[:, :, :], wk).then_inc(wk_loaded, 16)
            sp.dma_start(bk_s[:, :], bk).then_inc(wk_loaded, 16)
            load_ctx(0)
            sp.dma_start(wq_s[:, :, :], wq).then_inc(wq_loaded, 16)
            sp.dma_start(bq_s[:, :], bq).then_inc(wq_loaded, 16)
            for j in range(1, KC):
                load_ctx(j)
            sp.dma_start(wv_s[:, :, :], wv).then_inc(wv_loaded, 16)
            sp.dma_start(bv_s[:, :], bv.partition_broadcast(P)).then_inc(wv_loaded, 16)
            for c in range(1, NC):
                sp.dma_start(x_in[:, QT * c:QT * (c + 1), :], x_chunks[c]).then_inc(x_loaded[c], 16)

            def stage_k(g, parts=(0, 1, 2)):
                if parts[0] == 0:
                    wait(sp, k_staged, 6 * 16 * g)
                for part in parts:
                    sp.wait_ge(*((k_copied, 2 * KC) if g > 1 else (k_high, KC), (k_mid[g // 2], 1), (k_split[g // 2], 1))[part])
                    src = k_part[part][64 * (g % 2):64 * (g % 2) + 64, g // 2, :]
                    for r in range(6):
                        if K_PARTS[r] == part:
                            dst = k_stack[D * r:D * (r + 1), g % 2 * KSW:(g % 2 + 1) * KSW]
                            sp.dma_start(dst.rearrange("p (h n) -> p h n", h=HG), src).then_inc(k_staged, 16)

            def stage_q(s, parts=(0, 1, 2)):
                g, c = s // NC, s % NC
                if parts[0] == 0:
                    wait(sp, q_staged[s % 2], 6 * 16 * (s // 2))
                for part in parts:
                    sp.wait_ge(*((q_copied, 2 * c + 2) if c else (q_high, 1), (q_mid[c], 1), (q_split[c], 1))[part])
                    src = q_part[part][64 * (g % 2):64 * (g % 2) + 64, g // 2, c * QC:(c + 1) * QC]
                    for r in range(6):
                        if Q_PARTS[r] == part:
                            dst = q_stack[D * r:D * (r + 1), c * HG * QC:(c + 1) * HG * QC]
                            sp.dma_start(dst.rearrange("p (h n) -> p h n", h=HG), src).then_inc(q_staged[s % 2], 16)

            def stage_v(s):
                g = s // NC
                wait(sp, v_staged[s % 2], 16 * (s // 2))
                sp.dma_start(v_grp[s % 2][:, :], v_mem[:, g * VG:(g + 1) * VG]).then_inc(v_staged[s % 2], 16)

            for part in range(3):
                stage_k(0, [part])
                stage_q(0, [part])
            sp.dma_start(wo_s[:, :, :], wo).then_inc(wo_loaded, 16)
            sp.dma_start(bo_s[:, :], bo.partition_broadcast(P)).then_inc(wo_loaded, 16)
            sp.wait_ge(consts_made, 1)
            sp.dma_start(rt_w[:, :, 0:E + 1], router).then_inc(wo_loaded, 16)
            sp.dma_start(gates[:, 0:1], g_x.partition_broadcast(P)).then_inc(wo_loaded, 16)
            sp.dma_start(gates[:, 1:2], g_f.partition_broadcast(P)).then_inc(wo_loaded, 16)
            sp.wait_ge(v_copied, KT)
            stage_v(0)
            stage_q(1)
            stage_v(1)
            stage_q(2)
            stage_k(1)
            stage_q(3)
            for t in range(STEPS - 2):
                sp.wait_ge(pv_done, KT * (t + 1))
                stage_v(t + 2)
                if t + NC < STEPS:
                    stage_q(t + NC)
                if t + 1 in (NC, 2 * NC):
                    stage_k((t + 1) // NC + 1)
                if t + NC == STEPS - 1:
                    sp.wait_ge(q_staged[0], 6 * 16 * STEPS // 2)
                    sp.wait_ge(q_staged[1], 6 * 16 * STEPS // 2)
                    sp.wait_ge(k_staged, 6 * 16 * G)
                    for dst, src in (("gu0", gu[:, :, 0:E * I]), ("gu1", gu[:, :, E * I:]), ("dw0", dw[:, 0:E // 2, :]),
                                     ("dw1", dw[:, E // 2:, :]), ("sg", sg), ("su", su), ("sd", sd)):
                        sp.dma_start(w_raw[dst][:, :, :], src).then_inc(ffw_loaded, 16)

            x_c = x.rearrange("(c t p) n -> c p t n", c=NC, p=P)
            o_c = out.rearrange("(c t p) n -> c t p n", c=NC, p=P)
            big_c = big[:, :].rearrange("p (g c n) -> p g c n", g=G, c=NC)

            def load_chunk(c):
                wait(sp, x1_ready, QT * c)
                sp.dma_start(xb[:, :, :], x_c[c]).then_inc(xb_loaded, 16)
                sp.wait_ge(out_copied, STEPS - NC + c + 1)
                wait(sp, att_ready, QT * c)
                sp.dma_start(outT[:, :, :], big_c[:, :, c, :]).then_inc(outT_loaded, 16)

            def store_chunk(c):
                for t in range(QT):
                    sp.wait_ge(combined, c * QT * PAIRS + QT * (PAIRS - 1) + t + 1)
                    sp.dma_start(o_c[c, t], res[:, t, :]).then_inc(stored[t], 16)

            sp.wait_ge(v_staged[0], 16 * STEPS // 2)
            sp.wait_ge(v_staged[1], 16 * STEPS // 2)
            load_chunk(0)
            load_chunk(1)
            for c in range(NC):
                if c + 2 < NC:
                    load_chunk(c + 2)
                store_chunk(c)
            for t in range(QT):
                sp.wait_ge(stored[t], 16 * NC)

        @block.gpsimd
        def _(pool):
            done = [0]

            def link(ins):
                done[0] += 1
                ins.then_inc(pool_chain, 1)
                pool.wait_ge(pool_chain, done[0])

            link(nc.gpsimd.memset(ident[:, :], 0.0))
            link(nc.gpsimd.affine_select(out=ident[:, :], in_=ident[:, :], compare_op=ALU.not_equal, fill=1.0,
                                         base=0, pattern=[[-1, P]], channel_multiplier=1))
            link(nc.gpsimd.tensor_copy(ident_b[:, :], ident[:, :]))
            link(nc.gpsimd.memset(mhalf[:, :], -0.5))
            nc.gpsimd.memset(rt_w[:, :, :], 0.0).then_inc(consts_made, 1)
            pool.wait_ge(consts_made, 1)

            def rstd1_of(c):
                sl = slice(QT * c, QT * (c + 1))
                pool.wait_ge(ln1_stats, c + 1)
                link(nc.gpsimd.tensor_scalar(rstd1[:, sl], mv1[:, sl, 1], EPS, None, ALU.add))
                nc.gpsimd.tensor_tensor(rstd1[:, sl], rstd1[:, sl], mhalf[:, :], ALU.pow).then_inc(ln1_rstd, 1)
                pool.wait_ge(ln1_rstd, c + 1)

            rstd1_of(0)
            blocks = v_mem[:, :].rearrange("p (a w) -> p a w", w=VW)
            link(nc.gpsimd.memset(blocks[:, :, D:VW], 0.0))
            link(nc.gpsimd.memset(v_all[:, :, KT - 1, :, :], 0.0))
            nc.gpsimd.memset(blocks[:, :, D:D + 1], 1.0).then_inc(v_ones, 1)
            pool.wait_ge(v_ones, 1)
            def ones_of(i):
                nc.gpsimd.memset(k_stack[SPLIT:ROWS, i * NK:(i + 1) * NK], 1.0).then_inc(key_ones, 1)
                pool.wait_ge(key_ones, i + 1)

            for i in range(ONES_EARLY):
                ones_of(i)
            for e in range(E):
                link(nc.gpsimd.memset(iota[:, e:e + 1], float(e)))

            def shift_of(s, h):
                u = slice(QT * h, QT * (h + 1))
                hold(pool, head_max, HG * s + (h + 1), passed["pool"])
                nc.gpsimd.tensor_copy(shift[:, u, 0], neg_max[:, u]).then_inc(shift_high, 1)
                pool.wait_ge(shift_high, HG * s + (h + 1))
                nc.gpsimd.tensor_tensor(shift[:, u, 1], neg_max[:, u], shift[:, u, 0],
                                        ALU.subtract).then_inc(shift_low, 1)

            def take_high_off(what):
                full, hi, _, _ = parts_of(what)
                pool.wait_ge(*consumer(what))
                nc.gpsimd.tensor_tensor(full, full, hi, ALU.subtract).then_inc(split_sems(what)[0], 1)
                pool.wait_ge(split_sems(what)[0], 1)

            def low_part(what):
                full, _, mid, lo = parts_of(what)
                _, mid_written, low_written = split_sems(what)
                pool.wait_ge(mid_written, 1)
                nc.gpsimd.tensor_tensor(lo, full, mid, ALU.subtract).then_inc(low_written, 1)
                pool.wait_ge(low_written, 1)

            for kind, what in ORDER:
                if kind == "stats" and what:
                    rstd1_of(what)
                elif kind == "max":
                    shift_of(0, what)
                    pool.wait_ge(shift_low, what + 1)
                elif kind == "split" and what[0] == "q" and what[1] > 1:
                    take_high_off(what)
                elif kind == "mid":
                    low_part(what)
                elif kind == "p" and what[0] == "v":
                    k, w = what[1], KW[what[1]]
                    if k == 0:
                        pool.wait_ge(wv_loaded, 32)
                    pool.wait_ge(v_filled_out, k + 1)
                    v_tile = v_all[0:w, :, k, :, 0:D]
                    nc.gpsimd.tensor_tensor(v_tile, v_tile, bv_s[0:w, :].rearrange("p (g h d) -> p g h d", g=G, h=HG),
                                            ALU.add).then_inc(v_copied, 1)
                    pool.wait_ge(v_copied, k + 1)
                    if k < 2 * HG - ONES_EARLY:
                        ones_of(ONES_EARLY + k)
            take_high_off(LAST_K)
            low_part(LAST_K)
            with pool.Fori(1, STEPS) as s:
                for h in range(HG):
                    shift_of(s, h)

            pool.wait_ge(tanh_done, 1)
            nc.gpsimd.tensor_scalar(bo_s[:, :], bo_s[:, :], tg[:, 0:1], None, ALU.mult).then_inc(bo_scaled, 1)
            pool.wait_ge(bo_scaled, 1)

            def residual_input(c):
                pool.wait_ge(xb_loaded, 16 * c + 16)
                for t in range(QT):
                    nc.gpsimd.tensor_tensor(xb[:, t, :], xb[:, t, :], bo_s[:, :], ALU.add).then_inc(xb_ready, 1)

            def rstd2_of(c):
                hold(pool, ln2_stats, QT * c + QT, passed["pool"])
                nc.gpsimd.tensor_scalar(rstd2[:, :], mv2[:, :, 1], EPS, None, ALU.add).then_inc(ln2_eps, 1)
                pool.wait_ge(ln2_eps, c + 1)
                nc.gpsimd.tensor_tensor(rstd2[:, :], rstd2[:, :], mhalf[:, :], ALU.pow).then_inc(ln2_rstd, 1)

            def low_weights(n):
                pool.wait_ge(w_high, n + 1)
                w = W_SPLITS[n]
                nc.gpsimd.tensor_tensor(w_lo[w][:, :, :], w_raw[w][:, :, :], w_hi[w][:, :, :].bitcast(F32),
                                        ALU.subtract).then_inc(w_low, 1)

            def hidden_low_of(c, u):
                pool.wait_ge(hidden_high, UNITS * c + (u + 1))
                nc.gpsimd.tensor_tensor(hid_lo[:, u % 4, :], hid[u % 2][:, :], hid_hi[:, u % 4, :].bitcast(F32),
                                        ALU.subtract).then_inc(hidden_low, 1)

            residual_input(0)
            for n in range(len(W_SPLITS)):
                if n == 3:
                    rstd2_of(0)
                low_weights(n)

            def experts(c, next_m=True):
                if next_m:
                    residual_input(c + 1)
                for u in range(UNITS):
                    hidden_low_of(c, u)
                    if next_m and u == UNITS - 4:
                        rstd2_of(c + 1)

            experts(0)
            with pool.Fori(1, NC - 1) as c:
                experts(c)
            experts(NC - 1, False)

        @block.scalar
        def _(act):
            def copy_p(what):
                kind, n = what
                act.wait_ge(p_filled, PRO_AT[what] + 1)
                bank = bank_p[PRO_AT[what] % 4]
                if kind == "x":
                    wait(act, p_filled, PRO_AT.get(("q", n // 2 * 2 - 1), -1) + 1)
                    nc.scalar.copy(xnT[:, n % 2, :], bank).then_inc(xnT_copied, 1)
                    return
                if kind == "v":
                    if n == 0:
                        act.wait_ge(v_ones, 1)
                    w = KW[n]
                    nc.scalar.copy(v_all[0:w, :, n, :, 0:D], bank[0:w, 0:C].rearrange("p (g h d) -> p g h d", g=G, h=HG)
                                   ).then_inc(v_filled_out, 1)
                    return
                if kind == "k":
                    a, j = n // KC, n % KC
                    cols = slice(KP0[j], KP0[j] + KPW[j])
                    full, hi, bias, bank, sem_ = k_full[:, a, cols], k_part[0][:, a, cols], bk_s[:, a:a + 1], bank[:, 0:KPW[j]], k_copied
                else:
                    c, a = n // 2, n % 2
                    full, hi, bias, sem_ = q_full[:, c, a, :], q_part[0][:, a, c * QC:(c + 1) * QC], bq_s[:, a:a + 1], q_copied
                ins = nc.scalar.activation(full, bank, ACT.Identity, bias=bias)
                if (kind, n) > (kind, 1 if kind == "q" else KC - 1):
                    ins = nc.scalar.activation(hi, bank, ACT.Identity, bias=bias)
                ins.then_inc(sem_, 1)

            def middle_part(what):
                high_off, mid_written, _ = split_sems(what)
                act.wait_ge(high_off, 1)
                full, _, mid, _ = parts_of(what)
                nc.scalar.copy(mid, full).then_inc(mid_written, 1)

            act.wait_ge(wk_loaded, 32)
            act.wait_ge(wq_loaded, 32)

            def copy_shift(s, h):
                f = SHIFT_AT[h]
                act.wait_ge(a_filled, FILLS * s + (f + 1))
                nc.scalar.copy(queries(s, h, 0, QC, SPLIT, ROWS), ps_a[SPLIT:ROWS, f % 4, :]).then_inc(shift_copied, 1)

            for kind, what in ORDER:
                if kind == "a" and A_FILLS[what][0] == "shift":
                    copy_shift(0, A_FILLS[what][1])
                elif kind == "p":
                    copy_p(what)
                elif kind == "mid":
                    middle_part(what)
            for each in q_split:
                act.wait_ge(each, 1)
            act.wait_ge(wo_loaded, 16 * 5)
            nc.scalar.activation(tg[:, :], gates[:, :], ACT.Tanh).then_inc(tanh_done, 1)

            def copy_out(s):
                act.wait_ge(pv_done, KT * s + KT)
                nc.scalar.copy(out_at(s), ps_o[:, :]).then_inc(out_copied, 1)

            def copy_m(c, f):
                kind, t = M_ORDER[f]
                if kind == "attT":
                    act.wait_ge(m_filled, M_FILLS * c + (f + 1))
                    nc.scalar.copy(attT[:, :, t * P:(t + 1) * P],
                                   bank_m(c, f)[:, 0:2 * P].rearrange("p (a n) -> p a n", a=2)).then_inc(attT_ready, 1)
                elif kind == "xn2T":
                    act.wait_ge(m_filled, M_FILLS * c + (f + 1))
                    nc.scalar.copy(xn2T_hi[:, t, :], bank_m(c, f)).then_inc(xn2T_high, 1)
                elif kind == "router":
                    act.wait_ge(rneg_ready, c + 1)
                    for i in range(QT):
                        nc.scalar.activation(e8[:, i, :], logits[:, i, 0:E], ACT.Exp, bias=rneg[:, i:i + 1])
                    nc.scalar.activation(ez[:, :], logits[:, :, E], ACT.Exp, scale=-1.0).then_inc(router_exp, 1)

            def step(s, par, next_a, first=False, last=False):
                f = 0
                for k in range(KT):
                    for h in range(HG):
                        i = HG * k + h
                        act.wait_ge(b_filled, EXPS * s + (i + 1))
                        if h == 0 and not (first and k < 2):
                            act.wait_ge(pv_done, KT * s + (k - 1))
                        nc.scalar.activation(probs[0:KW[k], (k + par) % 2, h, :], ps_b[0:KW[k], b_bank(i, par), :],
                                             ACT.Exp, scale=SCALE).then_inc(exp_done, 1)
                        if last and h == 1 and LAST_PLACES[k][0] is not None:
                            copy_m(0, LAST_PLACES[k][0])
                    if k == 0 and not first:
                        copy_out(s - 1)
                    if k == 1 and first:
                        middle_part(LAST_K)
                    if next_a:
                        for kind, g, _ in A_FILLS[f:f + A_SHARE[k]]:
                            if kind == "shift":
                                copy_shift(s + 1, g)
                        f += A_SHARE[k]
                    if last and LAST_PLACES[k][1] is not None:
                        copy_m(0, LAST_PLACES[k][1])

            step(0, 0, True, first=True)
            with act.Fori(0, STEPS // 2 - 1) as j:
                step(j * 2 + 1, 1, True)
                step(j * 2 + 2, 0, True)
            step(STEPS - 1, 1, False, last=True)
            copy_out(STEPS - 1)

            def hidden_high_of(c, u):
                act.wait_ge(h_ready, UNITS * c + (u + 1))
                if not (isinstance(c, int) and c == 0 and u < 4):
                    act.wait_ge(d_filled, QT * PAIRS * c + QT * (u // 2 - 1))
                nc.scalar.copy(hid_hi[:, u % 4, :], hid[u % 2][:, :]).then_inc(hidden_high, 1)

            def experts(c, next_m=True, before=True):
                if before:
                    copy_m(c, M_AT["router", 0])
                for u in range(UNITS):
                    act.wait_ge(gu_filled, UNITS * c + (u + 1))
                    if not (isinstance(c, int) and c == 0 and u < 2):
                        act.wait_ge(h_ready, UNITS * c + (u - 1))
                    nc.scalar.activation(silu[:, u % 2, :], ps_a[:, 2 * (u % 2), :], ACT.Silu).then_inc(silu_done, 1)
                    if next_m and u == UNITS - 1:
                        copy_m(c + 1, M_AT["xn2T", 0])
                        copy_m(c + 1, M_AT["xn2T", 1])
                    hidden_high_of(c, u)
                    for f in M_AT_PLACE[u // 2][0:2] if u % 2 == 0 else M_AT_PLACE[u // 2][2:4]:
                        if next_m and f is not None:
                            copy_m(c + 1, f)

            experts(0, before=False)
            with act.Fori(1, NC - 1) as c:
                experts(c)
            experts(NC - 1, False)

        @block.vector
        def _(dve):
            done = [0, 0]

            def link(ins):
                done[0] += 1
                ins.then_inc(dve_chain, 1)
                hold(dve, dve_chain, done[1] + done[0], passed["dve"])

            def stats_of(c):
                dve.wait_ge(x_loaded[c], 16)
                wait(dve, ln1_stats, c)
                for t in range(QT):
                    nc.vector.bn_stats(stats[:, t, :], x_in[:, QT * c + t, :]).then_inc(dve_chain, 1)
                    done[0] += 1
                dve.wait_ge(dve_chain, done[0])
                for t in range(QT):
                    last = nc.vector.bn_aggr(mv1[:, QT * c + t, :], stats[:, t, :])
                last.then_inc(ln1_stats, 1)

            def norm1(c):
                dve.wait_ge(ln1_rstd, c + 1)
                for t in range(QT * c, QT * (c + 1)):
                    last = nc.vector.tensor_scalar(x_in[:, t, :], x_in[:, t, :], mv1[:, t, 0:1], rstd1[:, t:t + 1],
                                                   ALU.subtract, ALU.mult)
                last.then_inc(ln1_done, 1)

            def split(what):
                full, hi, mid, lo = parts_of(what)
                high_off, mid_written, low_written = split_sems(what)
                if what == FIRST_K:
                    for j in range(KC):
                        cols = slice(KP0[j], KP0[j] + KPW[j])
                        dve.wait_ge(k_copied, j + 1)
                        nc.vector.tensor_copy(hi[:, cols], full[:, cols]).then_inc(k_high, 1)
                        dve.wait_ge(k_high, j + 1)
                        ins = nc.vector.tensor_tensor(full[:, cols], full[:, cols], hi[:, cols], ALU.subtract)
                    ins.then_inc(high_off, 1)
                    return
                dve.wait_ge(*consumer(what))
                nc.vector.tensor_copy(hi, full).then_inc(q_high, 1)
                dve.wait_ge(q_high, 1)
                nc.vector.tensor_tensor(full, full, hi, ALU.subtract).then_inc(high_off, 1)
                dve.wait_ge(high_off, 1)
                nc.vector.tensor_copy(mid, full).then_inc(mid_written, 1)
                dve.wait_ge(mid_written, 1)
                nc.vector.tensor_tensor(lo, full, mid, ALU.subtract).then_inc(low_written, 1)

            def maximum(s, f):
                kind, u, j = A_FILLS[f]
                if kind == "shift":
                    return
                dve.wait_ge(a_filled, FILLS * s + (f + 1))
                n = KC * u + j
                nc.vector.reduce_max(piece_max[:, u, j:j + 1], ps_a[:, f % 4, 0:KPW[j]],
                                     axis=AX.X).then_inc(a_reduced, 1)
                if (n + 1) % (QT * KC) == 0:
                    h = u // QT
                    dve.wait_ge(a_reduced, HG * QT * KC * s + (n + 1))
                    nc.vector.tensor_reduce(neg_max[:, QT * h:QT * (h + 1)], piece_max[:, QT * h:QT * (h + 1), :],
                                            op=ALU.max, axis=AX.X, negate=True).then_inc(head_max, 1)

            for kind, what in ORDER:
                if kind == "stats":
                    stats_of(what)
                elif kind == "norm":
                    norm1(what)
                elif kind == "split" and what in (FIRST_K, ("q", 1)):
                    split(what)
                elif kind == "a":
                    maximum(0, what)
            with dve.Fori(1, STEPS) as s:
                for f in range(FILLS):
                    maximum(s, f)

            dve.wait_ge(wo_loaded, 16 * 5)
            link(nc.vector.tensor_copy(rt_parts[:, :, 0, :], rt_w[:, :, :]))
            nc.vector.tensor_tensor(rt_parts[:, :, 1, :], rt_w[:, :, :], rt_parts[:, :, 0, :].bitcast(F32),
                                    ALU.subtract).then_inc(rt_split, 1)
            dve.wait_ge(ffw_loaded, 16 * 7)
            dve.wait_ge(pv_done, KT * (STEPS - 1))

            def high_weights(n):
                w = W_SPLITS[n]
                nc.vector.tensor_copy(w_hi[w][:, :, :], w_raw[w][:, :, :]).then_inc(w_high, 1)

            def normalize(c, t):
                f = M_AT["att", t]
                dve.wait_ge(m_filled, M_FILLS * c + (f + 1))
                sums = bank_m(c, f).rearrange("p (h w) -> p h w", w=VW)
                link(nc.vector.reciprocal(rden[:, t, :], sums[:, :, D]))
                nc.vector.tensor_tensor(att[:, t, :].rearrange("p (h d) -> p h d", d=D), sums[:, :, 0:D],
                                        rden[:, t, :].unsqueeze(2).to_broadcast([P, H, D]), ALU.mult).then_inc(att_ready, 1)

            def residual(c, t):
                f = M_AT["proj", t]
                dve.wait_ge(m_filled, M_FILLS * c + (f + 1))
                dve.wait_ge(xb_ready, QT * c + (t + 1))
                nc.vector.scalar_tensor_tensor(x1[:, t, :], bank_m(c, f)[:, 0:C], tg[:, 0:1], xb[:, t, :],
                                               ALU.mult, ALU.add).then_inc(x1_ready, 1)
                dve.wait_ge(x1_ready, QT * c + (t + 1))
                link(nc.vector.bn_stats(stats[:, t, :], x1[:, t, :]))
                nc.vector.bn_aggr(mv2[:, t, :], stats[:, t, :]).then_inc(ln2_stats, 1)

            def norm2(c):
                dve.wait_ge(ln2_rstd, c + 1)
                for t in range(QT):
                    nc.vector.tensor_scalar(xn2[:, t, :], x1[:, t, :], mv2[:, t, 0:1], rstd2[:, t:t + 1],
                                            ALU.subtract, ALU.mult).then_inc(xn2_ready, 1)

            def xn2T_low_of(c, a):
                dve.wait_ge(xn2T_high, 2 * c + (a + 1))
                nc.vector.tensor_tensor(xn2T_lo[:, a, :], bank_m(c, M_AT["xn2T", a]), xn2T_hi[:, a, :].bitcast(F32),
                                        ALU.subtract).then_inc(xn2T_ready, 1)

            def logits_max(c):
                f = M_AT["router", 0]
                dve.wait_ge(m_filled, M_FILLS * c + (f + 1))
                sums = bank_m(c, f)[:, 0:ROUTE_W * QT].rearrange("p (t r e) -> p t e r", t=QT, r=2)
                nc.vector.tensor_reduce(logits[:, :, :], sums, op=ALU.add, axis=AX.X).then_inc(logits_ready, 1)
                dve.wait_ge(logits_ready, c + 1)
                nc.vector.tensor_reduce(rneg[:, :], logits[:, :, 0:E], op=ALU.max, axis=AX.X,
                                        negate=True).then_inc(rneg_ready, 1)

            def route_first(c):
                hold(dve, router_exp, c + 1, passed["dve"])
                for t in range(QT):
                    ins = nc.vector.max(v8[:, t, :], e8[:, t, :])
                link(ins)
                for t in range(QT):
                    ins = nc.vector.max_index(i8[:, t, :], v8[:, t, :], e8[:, t, :])
                nc.vector.tensor_tensor(s2[:, :, 0], v8[:, :, 0], v8[:, :, 1], ALU.add)
                link(nc.vector.tensor_scalar(s2[:, :, 1], ez[:, :], 1.0, None, ALU.add))

            def route(c):
                nc.vector.tensor_copy(i2[:, :, :], i8[:, :, 0:2])
                wait(dve, combined, QT * PAIRS * c)
                link(nc.vector.reciprocal(r2[:, :, :], s2[:, :, :]))
                nc.vector.tensor_tensor(cw2[:, :, :, :], iota[:, :].unsqueeze(1).unsqueeze(1).to_broadcast([P, QT, 2, E]),
                                        i2[:, :, :].unsqueeze(3).to_broadcast([P, QT, 2, E]), ALU.is_equal)
                link(nc.vector.tensor_scalar(r2[:, :, :], r2[:, :, :], tg[:, 1:2], None, ALU.mult))
                link(nc.vector.tensor_tensor(w2[:, :, :], v8[:, :, 0:2], r2[:, :, 0:1].to_broadcast([P, QT, 2]),
                                             ALU.mult))
                link(nc.vector.tensor_tensor(cw2[:, :, :, :], cw2[:, :, :, :],
                                             w2[:, :, :].unsqueeze(3).to_broadcast([P, QT, 2, E]), ALU.mult))
                link(nc.vector.tensor_tensor(cw[:, :, :], cw2[:, :, 0, :], cw2[:, :, 1, :], ALU.add))

            def hidden_of(c, u):
                dve.wait_ge(silu_done, UNITS * c + (u + 1))
                if not (isinstance(c, int) and c == 0 and u < 2):
                    dve.wait_ge(hidden_low, UNITS * c + (u - 1))
                nc.vector.tensor_tensor(hid[u % 2][:, :], silu[:, u % 2, :], ps_a[:, 2 * (u % 2) + 1, :],
                                        ALU.mult).then_inc(h_ready, 1)

            def combine(c, pair, t):
                d = QT * pair + t
                dve.wait_ge(d_filled, QT * PAIRS * c + (d + 1))
                if pair == 0:
                    wait(dve, stored[t], 16 * c)
                else:
                    dve.wait_ge(combined, QT * PAIRS * c + (d + 1 - QT))
                bank = bank_d[d % 2]
                so_far = x1 if pair == 0 else res
                if pair < E // 2:
                    link(nc.vector.scalar_tensor_tensor(res[:, t, :], bank[:, 0:C], cw[:, t, 2 * pair:2 * pair + 1],
                                                        so_far[:, t, :], ALU.mult, ALU.add))
                    ins = nc.vector.scalar_tensor_tensor(res[:, t, :], bank[:, C:2 * C],
                                                         cw[:, t, 2 * pair + 1:2 * pair + 2],
                                                         res[:, t, :], ALU.mult, ALU.add)
                else:
                    ins = nc.vector.scalar_tensor_tensor(res[:, t, :], bank[:, 0:C], r2[:, t, 1:2],
                                                         res[:, t, :], ALU.mult, ALU.add)
                ins.then_inc(combined, 1)

            def work_m(c, f):
                kind, t = M_ORDER[f]
                if kind == "att":
                    normalize(c, t)
                elif kind == "proj":
                    residual(c, t)

            def experts(c, next_m=True, before=True):
                if before:
                    logits_max(c)
                for pair in range(PAIRS):
                    def place(t):
                        if pair or before:
                            combine(c if pair else c - 1, (pair - 1) % PAIRS, t)
                        if next_m and M_AT_PLACE[pair][t] is not None:
                            work_m(c + 1, M_AT_PLACE[pair][t])

                    if pair == PAIRS - 1 and next_m:
                        norm2(c + 1)
                    hidden_of(c, 2 * pair)
                    place(0)
                    if pair < PAIRS - 1:
                        place(1)
                    hidden_of(c, 2 * pair + 1)
                    if pair == 0:
                        route_first(c)
                    if pair == PAIRS - 1 and next_m:
                        xn2T_low_of(c + 1, 0)
                        xn2T_low_of(c + 1, 1)
                    if pair == PAIRS - 1:
                        place(1)
                    place(2)
                    place(3)
                    if pair == 0:
                        route(c)

            dve.wait_ge(tanh_done, 1)
            for f in range(M_AT["xn2T", 0]):
                if f % 2 == 0:
                    high_weights(f // 2)
                work_m(0, f)
            for n in range(M_AT["xn2T", 0] // 2, len(W_SPLITS)):
                high_weights(n)
            norm2(0)
            xn2T_low_of(0, 0)
            xn2T_low_of(0, 1)
            logits_max(0)
            before_chunk = done[0]
            experts(0, before=False)
            start, per_chunk = done[0], done[0] - before_chunk
            with dve.Fori(1, NC - 1) as c:
                done[0], done[1] = 0, (c - 1) * per_chunk + start
                experts(c)
            done[0], done[1] = start + (NC - 2) * per_chunk, 0
            experts(NC - 1, False)
            for t in range(QT):
                combine(NC - 1, PAIRS - 1, t)

        @block.tensor
        def _(pe):
            mm = nc.tensor.matmul

            def transpose(out_, in_):
                return mm(out_, in_, ident[:, :], start=True, stop=True, is_transpose=True)

            def project(what):
                kind, n = what
                at_ = PRO_AT[what]
                bank = bank_p[at_ % 4]
                if at_ >= 4:
                    pe.wait_ge(*consumer(P_FILLS[at_ - 4]))
                if kind == "k":
                    a, j = n // KC, n % KC
                    if a == 0:
                        pe.wait_ge(wk_loaded, 32)
                        pe.wait_ge(ctx_loaded[j], 16)
                    for i in range(2):
                        last = mm(bank[:, 0:KPW[j]], wk_s[:, i, a * P:(a + 1) * P],
                                  ctx_in[:, i, KP0[j]:KP0[j] + KPW[j]], start=(i == 0), stop=(i == 1))
                elif kind == "x":
                    c, a = n // 2, n % 2
                    pe.wait_ge(consts_made, 1)
                    pe.wait_ge(ln1_done, c + 1)
                    for t in range(QT):
                        last = transpose(bank[:, t * P:(t + 1) * P], x_in[:, QT * c + t, a * P:(a + 1) * P])
                elif kind == "q":
                    c, a = n // 2, n % 2
                    pe.wait_ge(wq_loaded, 32)
                    pe.wait_ge(xnT_copied, 2 * c + 2)
                    for i in range(2):
                        last = mm(bank, wq_s[:, i, a * P:(a + 1) * P], xnT[:, i, :], start=(i == 0), stop=(i == 1))
                else:
                    pe.wait_ge(wv_loaded, 32)
                    for i in range(2):
                        last = mm(bank[0:KW[n], 0:C], ctx_in[:, i, n * P:n * P + KW[n]], wv_s[:, i, :],
                                  start=(i == 0), stop=(i == 1))
                last.then_inc(p_filled, 1)

            def fill_a(s, f, first=False):
                kind, u, j = A_FILLS[f]
                if not (first and f < 4):
                    back, prev = (0, f - 4) if f >= 4 else (1, f - 4 + FILLS)
                    pkind, pu, pj = A_FILLS[prev]
                    if pkind == "score":
                        pe.wait_ge(a_reduced, HG * QT * KC * s + (KC * pu + pj + 1 - back * HG * QT * KC))
                    else:
                        pe.wait_ge(shift_copied, HG * s + (pu + 1 - back * HG))
                if kind == "score":
                    h, t = u // QT, u % QT
                    mm(ps_a[:, f % 4, 0:KPW[j]], queries(s, h, t * P, P, 0, SPLIT), keys(s, h, KP0[j], KPW[j], SPLIT),
                       start=True, stop=True).then_inc(a_filled, 1)
                else:
                    pe.wait_ge(shift_low, HG * s + (u + 1))
                    for t in range(QT):
                        last = mm(ps_a[SPLIT:ROWS, f % 4, t * P:(t + 1) * P], shift[:, QT * u + t, :], ident_b[:, :],
                                  start=True, stop=True)
                    last.then_inc(a_filled, 1)

            def begin_a(s, par):
                pe.wait_ge(q_staged[par], 6 * 16 * (s // 2) + 6 * 16)
                pe.wait_ge(k_staged, 6 * 16 * (s // NC) + 6 * 16)

            def probs_times_v(s, par, k, first=False):
                pe.wait_ge(exp_done, EXPS * s + HG * (k + 1))
                if k == 0:
                    pe.wait_ge(v_staged[par], 16 * (s // 2) + 16)
                    if not first:
                        pe.wait_ge(out_copied, s)
                for h in range(HG):
                    last = mm(ps_o[VW * h:VW * (h + 1), :], v_use[par][0:KW[k], k, h, :],
                              probs[0:KW[k], (k + par) % 2, h, :], start=(k == 0), stop=(k == KT - 1))
                last.then_inc(pv_done, 1)

            def step(s, par, next_a, first=False, last=False):
                if next_a:
                    begin_a(s + 1, 1 - par)
                f = 0
                for k in range(KT):
                    share = A_SHARE[k] if next_a else 0
                    for h in range(HG):
                        i = HG * k + h
                        if not first or b_bank_used(i, par) > 0:
                            pe.wait_ge(exp_done, EXPS * s + b_bank_used(i, par))
                        if k == 0:
                            pe.wait_ge(shift_copied, HG * s + (h + 1))
                        mm(ps_b[0:KW[k], b_bank(i, par), :], keys(s, h, k * P, KW[k]), queries(s, h, 0, QC),
                           start=True, stop=True).then_inc(b_filled, 1)
                        n = share * (h + 1) // HG
                        while share > 1 and f < sum(A_SHARE[:k]) + n:
                            fill_a(s + 1, f)
                            f += 1
                        if last and h == 1 and LAST_PLACES[k][0] is not None:
                            fill_m(0, LAST_PLACES[k][0])
                        if h == (2 if last or share <= 1 else HG - 1):
                            if k:
                                probs_times_v(s, par, k - 1, first)
                            elif not first:
                                probs_times_v(s - 1, 1 - par, KT - 1)
                    if share == 1:
                        fill_a(s + 1, f)
                        f += 1
                    if last and LAST_PLACES[k][1] is not None:
                        fill_m(0, LAST_PLACES[k][1])

            def fill_m(c, f):
                kind, t = M_ORDER[f]
                if isinstance(c, int) and c < 2 and f < 2:
                    if c == 0:
                        pe.wait_ge(a_reduced, HG * QT * KC * STEPS)
                        pe.wait_ge(shift_copied, HG * STEPS)
                        pe.wait_ge(outT_loaded, 16)
                        pe.wait_ge(wo_loaded, 16 * 5)
                        pe.wait_ge(rt_split, 1)
                    else:
                        pe.wait_ge(out_copied, STEPS)
                else:
                    back, prev = (0, f - 2) if f >= 2 else (1, max(g for g in range(M_FILLS) if g % 2 == f % 2))
                    pkind, pt = M_ORDER[prev]
                    gone, each = {"att": (att_ready, QT), "attT": (attT_ready, QT), "proj": (x1_ready, QT),
                                  "xn2T": (xn2T_ready, 2), "router": (router_exp, 1)}[pkind]
                    pe.wait_ge(gone, each * c + (pt + 1 - back * each))
                bank = bank_m(c, f)
                if kind == "att":
                    pe.wait_ge(outT_loaded, 16 * c + 16)
                    for g in range(G):
                        last = transpose(bank[:, g * P:(g + 1) * P], outT[:, g, t * P:(t + 1) * P])
                elif kind == "attT":
                    pe.wait_ge(att_ready, QT * c + (t + 1))
                    for a in range(2):
                        last = transpose(bank[:, a * P:(a + 1) * P], att[:, t, a * P:(a + 1) * P])
                elif kind == "proj":
                    pe.wait_ge(attT_ready, QT * c + (t + 1))
                    for a in range(2):
                        last = mm(bank[:, 0:C], attT[:, a, t * P:(t + 1) * P], wo_s[:, a, :],
                                  start=(a == 0), stop=(a == 1))
                elif kind == "xn2T":
                    pe.wait_ge(xn2_ready, QT * c + QT)
                    for i in range(QT):
                        last = transpose(bank[:, i * P:(i + 1) * P], xn2[:, i, t * P:(t + 1) * P])
                else:
                    pe.wait_ge(xn2T_ready, 2 * c + 2)
                    for i in range(QT):
                        for a in range(2):
                            for n, xx in enumerate((xn2T_hi, xn2T_lo)):
                                last = mm(bank[:, ROUTE_W * i:ROUTE_W * (i + 1)], xx[:, a, i * P:(i + 1) * P],
                                          rt_parts[:, a, :, :], start=(a == n == 0), stop=(a == n == 1))
                last.then_inc(m_filled, 1)

            for kind, what in ORDER:
                if kind == "a":
                    if what == 0:
                        begin_a(0, 0)
                    fill_a(0, what, first=True)
                elif kind == "p":
                    project(what)
            pe.wait_ge(key_ones, 2 * HG)
            for what in P_FILLS[-4:]:
                pe.wait_ge(*consumer(what))
            step(0, 0, True, first=True)
            with pe.Fori(0, STEPS // 2 - 1) as j:
                step(j * 2 + 1, 1, True)
                step(j * 2 + 2, 0, True)
            step(STEPS - 1, 1, False, last=True)
            probs_times_v(STEPS - 1, 1, KT - 1)

            def gate_up(c, u, n):
                if n == 0:
                    if not (isinstance(c, int) and c == 0 and u < 2):
                        pe.wait_ge(h_ready, UNITS * c + (u - 1))
                    if u == 0:
                        pe.wait_ge(xn2T_ready, 2 * c + 2)
                    if isinstance(c, int) and c == 0:
                        if u == 1:
                            pe.wait_ge(router_exp, 1)
                        pe.wait_ge(w_low, 1 if u < 4 else 3 if u < E else 6)
                name = ("gu0" if u < E // 2 else "gu1") if u < E else ("sg", "su")[n]
                at_ = 2 * I * (u % (E // 2)) + I * n if u < E else P * (u - E)
                for a in range(2):
                    for m, (ww, xx) in enumerate(((w_hi, xn2T_hi), (w_hi, xn2T_lo), (w_lo, xn2T_hi))):
                        last = mm(ps_a[:, 2 * (u % 2) + n, :], ww[name][:, a, at_:at_ + P], xx[:, a, :],
                                  start=(a == m == 0), stop=(a == 1 and m == 2))
                if n:
                    last.then_inc(gu_filled, 1)

            def down(c, pair, t):
                if t == 0:
                    pe.wait_ge(hidden_low, UNITS * c + 2 * (pair + 1))
                    if isinstance(c, int) and c == 0:
                        pe.wait_ge(w_low, 2 if pair < 2 else 4 if pair < 4 else 7)
                d = QT * pair + t
                if not (isinstance(c, int) and c == 0 and d < 2):
                    pe.wait_ge(combined, QT * PAIRS * c + (d - 1))
                for n in range(2):
                    u = 2 * pair + n
                    name = ("dw0" if u < E // 2 else "dw1") if u < E else "sd"
                    row = u % (E // 2) if u < E else u - E
                    cols = slice(n * C, (n + 1) * C) if u < E else slice(0, C)
                    for m, (hh, ww) in enumerate(((hid_hi, w_hi), (hid_hi, w_lo), (hid_lo, w_hi))):
                        last = mm(bank_d[d % 2][:, cols], hh[:, u % 4, t * P:(t + 1) * P], ww[name][:, row, :],
                                  start=(m == 0 and (u < E or n == 0)), stop=(m == 2 and (u < E or n == 1)))
                last.then_inc(d_filled, 1)

            def experts(c, next_m=True, before=True):
                for pair in range(PAIRS):
                    def place(t):
                        if pair or before:
                            down(c if pair else c - 1, (pair - 1) % PAIRS, t)
                        if next_m and M_AT_PLACE[pair][t] is not None:
                            fill_m(c + 1, M_AT_PLACE[pair][t])

                    gate_up(c, 2 * pair, 0)
                    if pair == 0 and before:
                        fill_m(c, M_AT["router", 0])
                    gate_up(c, 2 * pair, 1)
                    place(0)
                    gate_up(c, 2 * pair + 1, 0)
                    if pair < PAIRS - 1:
                        place(1)
                    gate_up(c, 2 * pair + 1, 1)
                    if pair == PAIRS - 1:
                        if next_m:
                            fill_m(c + 1, M_AT["xn2T", 0])
                            fill_m(c + 1, M_AT["xn2T", 1])
                        place(1)
                    place(2)
                    place(3)

            experts(0, before=False)
            with pe.Fori(1, NC - 1) as c:
                experts(c)
            experts(NC - 1, False)
            for t in range(QT):
                down(NC - 1, PAIRS - 1, t)


def kernel(x, ctx_1024, g_xattn, g_ffn, L0_xattn_Wq, L0_xattn_bq, L0_xattn_Wk, L0_xattn_bk, L0_xattn_Wv,
           L0_xattn_bv, L0_xattn_Wo, L0_xattn_bo, L0_ffn_router_weight, L0_ffn_gate_up_proj, L0_ffn_down_proj,
           L0_ffn_shared_gate_w, L0_ffn_shared_up_w, L0_ffn_shared_down_w, L0_ffn_shared_expert_gate_w):
    import numpy as np
    import concourse.bacc as bacc
    from concourse.bass_utils import run_bass_kernel_spmd

    def cols(w):
        w = np.asarray(w)
        return np.ascontiguousarray(w.T.reshape(-1, P, w.shape[0]).transpose(1, 0, 2))

    order = np.arange(C).reshape(2, 2, HG, D).transpose(0, 1, 3, 2).reshape(-1)
    arrays = {
        "x": np.ascontiguousarray(np.asarray(x)[0]),
        "ctxT": np.ascontiguousarray(np.asarray(ctx_1024)[0].T.reshape(2, P, NK).transpose(1, 0, 2)),
        "wq": cols(np.asarray(L0_xattn_Wq)[order]), "wk": cols(np.asarray(L0_xattn_Wk)[order]),
        "wv": cols(L0_xattn_Wv), "wo": cols(L0_xattn_Wo),
        "bq": np.ascontiguousarray(np.asarray(L0_xattn_bq)[order].reshape(2, P).T),
        "bk": np.ascontiguousarray(np.asarray(L0_xattn_bk)[order].reshape(2, P).T),
        "bv": np.asarray(L0_xattn_bv), "bo": np.asarray(L0_xattn_bo),
        "g_x": np.asarray(g_xattn), "g_f": np.asarray(g_ffn),
        "router": cols(np.concatenate([np.asarray(L0_ffn_router_weight), np.asarray(L0_ffn_shared_expert_gate_w)])),
        "gu": cols(np.asarray(L0_ffn_gate_up_proj).reshape(E * 2 * I, C)),
        "dw": np.ascontiguousarray(np.asarray(L0_ffn_down_proj).transpose(2, 0, 1)),
        "sg": cols(L0_ffn_shared_gate_w), "su": cols(L0_ffn_shared_up_w), "sd": cols(L0_ffn_shared_down_w),
    }
    nc = bacc.Bacc("TRN2", target_bir_lowering=False, num_devices=1)
    aps = [nc.dram_tensor(f"in_{n}", a.shape, mybir.dt.from_np(a.dtype), kind="ExternalInput").ap()
           for n, a in arrays.items()]
    result = nc.dram_tensor("result", (NT, C), F32, kind="ExternalOutput").ap()
    flamingo_block(nc, *aps, result)
    got = run_bass_kernel_spmd(nc, [{f"in_{n}": a for n, a in arrays.items()}], core_ids=[0])
    return got.results[0]["result"].reshape(1, NT, C)
```
